# Optimizing a Trainium2 kernel written in Bass

```python
import numpy as np
import jax
import jax.numpy as jnp

def _softmax(x, axis=-1):
    return jax.nn.softmax(x, axis=axis)

def _gelu(x):
    return jax.nn.gelu(x, approximate=True)

def _silu(x):
    return jax.nn.silu(x)

def _sigmoid(x):
    return jax.nn.sigmoid(x)

def _layernorm(x, axis=-1, eps=1e-05):
    m = jnp.mean(x, axis=axis, keepdims=True)
    v = jnp.var(x, axis=axis, keepdims=True)
    return (x - m) / jnp.sqrt(v + eps)

def _scatter_add(tgt, idx, src, axis=0):
    return tgt.at[idx].add(src)

def _segment_sum(src, seg, n):
    return jax.ops.segment_sum(src, seg, n)
kernel_name = 'mk_decoder_preln_d1_seqx_r8_90b70a'

def setup_inputs(seed: int=0):
    np.random.seed(seed)
    _w = jnp.asarray

    def _rec_inputs():
        import jax
        import jax.numpy as jnp
        _rk = jax.random.key(seed)
        x = -0.0003929 + 0.9999 * jax.random.normal(jax.random.fold_in(_rk, 1), (8, 56, 128), jnp.float32)
        _lenS = 56 - jax.random.randint(jax.random.fold_in(_rk, 7), (8,), 0, max(1, 56 // 4) + 1, jnp.int32)
        _lenS2 = 1500 - jax.random.randint(jax.random.fold_in(_rk, 8), (8,), 0, max(1, 1500 // 4) + 1, jnp.int32)
        _ctx_1024P = jax.random.normal(jax.random.fold_in(_rk, 11), (8, 16, 128), jnp.float32)
        _ctx_1024c = jax.random.dirichlet(jax.random.fold_in(_rk, 511), 0.3 * jnp.ones((16,), jnp.float32), (8, 1500))
        _ctx_1024t = jnp.einsum('bsk,bkd->bsd', _ctx_1024c, _ctx_1024P)
        _ctx_1024t = _ctx_1024t * jax.lax.rsqrt(jnp.mean(jnp.square(_ctx_1024t)) + 1e-12) * 0.953939
        ctx_1024 = 2.81802e-05 + 1.00001 * (_ctx_1024t + 0.3 * jax.random.normal(jax.random.fold_in(_rk, 611), (8, 1500, 128), jnp.float32))
        return (x, ctx_1024)
    x, ctx_1024 = _rec_inputs()

    def _L0_attn_setup():
        import jax, jax.numpy as jnp
        import numpy as np
        N_EMBD = 128
        N_HEAD = 16
        HEAD_DIM = N_EMBD // N_HEAD
        KV_RANK = 32
        Q_RANK = 64
        ROPE_DIM = 32
        B, T = (2, 256)
        EPS = 1e-06

        def _rope_tables(T, dim):
            inv_freq = 1.0 / 10000.0 ** (np.arange(0, dim, 2, dtype=np.float32) / dim)
            t = np.arange(T, dtype=np.float32)
            freqs = np.outer(t, inv_freq)
            emb = np.concatenate([freqs, freqs], -1)
            return (jnp.asarray(np.cos(emb)), jnp.asarray(np.sin(emb)))

        def _apply_rope(x, cos, sin):
            d2 = x.shape[-1] // 2
            x1, x2 = (x[..., :d2], x[..., d2:])
            rot = jnp.concatenate([-x2, x1], axis=-1)
            return x * cos[None, None, :, :] + rot * sin[None, None, :, :]
        key = jax.random.key(seed)
        ks = jax.random.split(key, 10)

        def w(k, fan_in, fan_out):
            return jax.random.normal(k, (fan_in, fan_out), dtype=jnp.float32) * fan_in ** (-0.5)
        return {'x': jax.random.normal(ks[0], (B, T, N_EMBD), dtype=jnp.float32), 'W_kv': w(ks[1], N_EMBD, KV_RANK), 'g_kv': jnp.ones((KV_RANK,), dtype=jnp.float32), 'W_kdec': w(ks[2], KV_RANK, N_HEAD * HEAD_DIM), 'W_vdec': w(ks[3], KV_RANK, N_HEAD * HEAD_DIM), 'W_q': w(ks[4], N_EMBD, Q_RANK), 'W_qdec': w(ks[5], Q_RANK, N_HEAD * HEAD_DIM), 'W_krope': w(ks[6], N_EMBD, N_HEAD * ROPE_DIM), 'W_qrope': w(ks[7], Q_RANK, N_HEAD * ROPE_DIM), 'W_o': w(ks[8], N_HEAD * HEAD_DIM, N_EMBD)}
    _L0_attn_all = _L0_attn_setup()
    _L0_attn_in = {k: v for k, v in _L0_attn_all.items() if k in ('W_kv', 'g_kv', 'W_kdec', 'W_vdec', 'W_q', 'W_qdec', 'W_krope', 'W_qrope', 'W_o')}
    del _L0_attn_all

    def _L0_xattn_setup():
        import jax, jax.numpy as jnp
        import numpy as np
        import math
        B, L, D = (4, 512, 128)
        M = 32
        EPS = 1e-06
        key = jax.random.key(seed)
        kq, kk, kv, kp = jax.random.split(key, 4)
        Q = jax.random.normal(kq, (B, L, D), dtype=jnp.float32)
        K = jax.random.normal(kk, (B, L, D), dtype=jnp.float32)
        V = jax.random.normal(kv, (B, L, D), dtype=jnp.float32)
        projection = jax.random.normal(kp, (M, D), dtype=jnp.float32)
        return {'Q': Q, 'K': K, 'V': V, 'projection': projection}
    _L0_xattn_all = _L0_xattn_setup()
    _L0_xattn_in = {k: v for k, v in _L0_xattn_all.items() if k in ('projection',)}
    del _L0_xattn_all

    def _L0_ffn_setup():
        import jax, jax.numpy as jnp
        import numpy as np
        B, T, D, H, E, TOPK = (2, 256, 128, 512, 8, 2)

        def sq_relu(x):
            return jnp.square(jax.nn.relu(x))
        key = jax.random.key(seed)
        ks = jax.random.split(key, 6)
        s = 0.02
        return {'x': jax.random.normal(ks[0], (B, T, D), dtype=jnp.float32), 'W_router': jax.random.normal(ks[1], (D, E), dtype=jnp.float32) * s, 'W_up': jax.random.normal(ks[2], (E, D, H), dtype=jnp.float32) * s, 'W_down': jax.random.normal(ks[3], (E, H, D), dtype=jnp.float32) * s, 'W_sh_up': jax.random.normal(ks[4], (D, H), dtype=jnp.float32) * s, 'W_sh_down': jax.random.normal(ks[5], (H, D), dtype=jnp.float32) * s}
    _L0_ffn_all = _L0_ffn_setup()
    _L0_ffn_in = {k: v for k, v in _L0_ffn_all.items() if k in ('W_router', 'W_up', 'W_down', 'W_sh_up', 'W_sh_down')}
    del _L0_ffn_all
    return {'x': x, 'ctx_1024': ctx_1024, 'L0_attn_W_kv': _L0_attn_in['W_kv'], 'L0_attn_g_kv': _L0_attn_in['g_kv'], 'L0_attn_W_kdec': _L0_attn_in['W_kdec'], 'L0_attn_W_vdec': _L0_attn_in['W_vdec'], 'L0_attn_W_q': _L0_attn_in['W_q'], 'L0_attn_W_qdec': _L0_attn_in['W_qdec'], 'L0_attn_W_krope': _L0_attn_in['W_krope'], 'L0_attn_W_qrope': _L0_attn_in['W_qrope'], 'L0_attn_W_o': _L0_attn_in['W_o'], 'L0_xattn_projection': _L0_xattn_in['projection'], 'L0_ffn_W_router': _L0_ffn_in['W_router'], 'L0_ffn_W_up': _L0_ffn_in['W_up'], 'L0_ffn_W_down': _L0_ffn_in['W_down'], 'L0_ffn_W_sh_up': _L0_ffn_in['W_sh_up'], 'L0_ffn_W_sh_down': _L0_ffn_in['W_sh_down']}

def reference(x, ctx_1024, L0_attn_W_kv, L0_attn_g_kv, L0_attn_W_kdec, L0_attn_W_vdec, L0_attn_W_q, L0_attn_W_qdec, L0_attn_W_krope, L0_attn_W_qrope, L0_attn_W_o, L0_xattn_projection, L0_ffn_W_router, L0_ffn_W_up, L0_ffn_W_down, L0_ffn_W_sh_up, L0_ffn_W_sh_down):
    import jax
    import jax.numpy as jnp

    def _L0_attn_ref(x, W_kv, g_kv, W_kdec, W_vdec, W_q, W_qdec, W_krope, W_qrope, W_o):
        import jax, jax.numpy as jnp
        import numpy as np
        N_EMBD = 128
        N_HEAD = 16
        HEAD_DIM = N_EMBD // N_HEAD
        KV_RANK = 32
        Q_RANK = 64
        ROPE_DIM = 32
        B, T = (2, 256)
        EPS = 1e-06

        def _rope_tables(T, dim):
            inv_freq = 1.0 / 10000.0 ** (np.arange(0, dim, 2, dtype=np.float32) / dim)
            t = np.arange(T, dtype=np.float32)
            freqs = np.outer(t, inv_freq)
            emb = np.concatenate([freqs, freqs], -1)
            return (jnp.asarray(np.cos(emb)), jnp.asarray(np.sin(emb)))

        def _apply_rope(x, cos, sin):
            d2 = x.shape[-1] // 2
            x1, x2 = (x[..., :d2], x[..., d2:])
            rot = jnp.concatenate([-x2, x1], axis=-1)
            return x * cos[None, None, :, :] + rot * sin[None, None, :, :]
        Bx, Tx, C = x.shape
        kv_c = x @ W_kv
        kv_c = kv_c * jax.lax.rsqrt(jnp.mean(kv_c * kv_c, axis=-1, keepdims=True) + EPS) * g_kv
        q_c = x @ W_q

        def heads(y, d):
            return y.reshape(Bx, Tx, N_HEAD, d).transpose(0, 2, 1, 3)
        k_content = heads(kv_c @ W_kdec, HEAD_DIM)
        v = heads(kv_c @ W_vdec, HEAD_DIM)
        q_content = heads(q_c @ W_qdec, HEAD_DIM)
        k_rope = heads(x @ W_krope, ROPE_DIM)
        q_rope = heads(q_c @ W_qrope, ROPE_DIM)
        cos, sin = _rope_tables(Tx, ROPE_DIM)
        q_rope = _apply_rope(q_rope, cos, sin)
        k_rope = _apply_rope(k_rope, cos, sin)
        q = jnp.concatenate([q_content, q_rope], axis=-1)
        k = jnp.concatenate([k_content, k_rope], axis=-1)
        scale = 1.0 / jnp.sqrt(jnp.float32(q.shape[-1]))
        scores = jnp.einsum('bhqd,bhkd->bhqk', q, k) * scale
        causal = jnp.tril(jnp.ones((Tx, Tx), dtype=bool))
        scores = jnp.where(causal[None, None], scores, jnp.float32(-jnp.inf))
        attn = jax.nn.softmax(scores, axis=-1)
        out = jnp.einsum('bhqk,bhkd->bhqd', attn, v)
        out = out.transpose(0, 2, 1, 3).reshape(Bx, Tx, N_HEAD * HEAD_DIM)
        return out @ W_o

    def _L0_xattn_ref(Q, K, V, projection):
        import jax, jax.numpy as jnp
        import numpy as np
        import math
        B, L, D = (4, 512, 128)
        M = 32
        EPS = 1e-06
        d_model = Q.shape[-1]
        m = projection.shape[0]
        inv_sqrt_d = 1.0 / math.sqrt(d_model)
        rf_q = jnp.exp(jnp.einsum('bld,md->blm', Q * inv_sqrt_d, projection)) / math.sqrt(m)
        rf_k = jnp.exp(jnp.einsum('bld,md->blm', K * inv_sqrt_d, projection))
        KV = jnp.einsum('blm,bld->bmd', rf_k, V)
        Z = jnp.sum(rf_k, axis=1)
        out = jnp.einsum('blm,bmd->bld', rf_q, KV)
        normalizer = jnp.einsum('blm,bm->bl', rf_q, Z) + EPS
        return out / normalizer[..., None]

    def _L0_ffn_ref(x, W_router, W_up, W_down, W_sh_up, W_sh_down):
        import jax, jax.numpy as jnp
        import numpy as np
        B, T, D, H, E, TOPK = (2, 256, 128, 512, 8, 2)

        def sq_relu(x):
            return jnp.square(jax.nn.relu(x))
        Bb, Tt, Dd = x.shape
        x_flat = x.reshape(-1, Dd)
        N = x_flat.shape[0]
        logits = x_flat @ W_router
        probs = jax.nn.sigmoid(logits)
        topk_probs, topk_idx = jax.lax.top_k(probs, TOPK)
        topk_probs = topk_probs / (jnp.sum(topk_probs, axis=-1, keepdims=True) + 1e-06)
        combine = jnp.zeros((N, E), dtype=x.dtype).at[jnp.arange(N)[:, None], topk_idx].add(topk_probs)
        out = sq_relu(x_flat @ W_sh_up) @ W_sh_down
        for e in range(E):
            h = sq_relu(x_flat @ W_up[e])
            out = out + combine[:, e:e + 1] * (h @ W_down[e])
        return out.reshape(Bb, Tt, Dd)
    x = x + _L0_attn_ref(_layernorm(x, axis=-1), L0_attn_W_kv, L0_attn_g_kv, L0_attn_W_kdec, L0_attn_W_vdec, L0_attn_W_q, L0_attn_W_qdec, L0_attn_W_krope, L0_attn_W_qrope, L0_attn_W_o)
    x = x + _L0_xattn_ref(_layernorm(x, axis=-1), ctx_1024, ctx_1024, L0_xattn_projection)
    x = x + _L0_ffn_ref(_layernorm(x, axis=-1), L0_ffn_W_router, L0_ffn_W_up, L0_ffn_W_down, L0_ffn_W_sh_up, L0_ffn_W_sh_down)
    return x

_drawn_inputs = setup_inputs


def setup_inputs(seed=0):
    import zlib

    import numpy as np

    out = dict(_drawn_inputs(seed))
    spreads = {'L0_attn_g_kv': (1.0, 0.2)}
    factors = {'L0_ffn_W_router': 3.853,
     'L0_ffn_W_up': 3.716,
     'L0_ffn_W_down': 3.391,
     'L0_ffn_W_sh_up': 3.259,
     'L0_ffn_W_sh_down': 2.92}
    for name, (base, spread) in spreads.items():
        noise = np.random.default_rng([zlib.crc32(name.encode()), seed]).standard_normal(out[name].shape)
        drawn = base * np.exp(spread * noise) if base else spread * noise
        out[name] = jnp.asarray(drawn.astype(out[name].dtype))
    for name, factor in factors.items():
        out[name] = (out[name] * factor).astype(out[name].dtype)
    return out
```

```python
from contextlib import ExitStack

import concourse.bass as bass
from concourse import mybir
import numpy as np

F32 = mybir.dt.float32
U32 = mybir.dt.uint32
ALU = mybir.AluOpType
ACT = mybir.ActivationFunctionType
AX_X = mybir.AxisListType.X

B, T, D = 8, 56, 128
H, HD, RD = 16, 8, 32
KVR, QR = 32, 64
L, M = 1500, 32
E, HID = 8, 512
LN_EPS, RMS_EPS, XN_EPS, TOPK_EPS = 1e-5, 1e-6, 1e-6, 1e-6

SLOT = 64
PAIRS = B // 2
QK = HD + RD
HP = H // 2
VW = HD + 1
NT = B * T
CT = 12
CP = L // CT
RING = 4
CHUNKS = HID // 128
NCH = (E + 1) * CHUNKS
NEG = -3.0e38

W128 = dict(ident=128, xpad=PAIRS * 128, wkv=KVR, wq=QR, krope=H * RD, wo=D, proj=M, router=E, mask=T, cos=RD, sin=RD, iota=E)
COL = {}
for _k, _n in W128.items():
    COL[_k] = (sum(v for v in list(W128.values())[:len(COL)]), _n)
N_A = sum(W128[k] for k in ("ident", "xpad", "wkv", "wq"))
N_W = sum(W128.values())


def decoder_layer(nc, pack128, wqcat, pack32, ctx_nat, ctx_tr, w_up, w_down, out):
    with ExitStack() as stack:
        def sb(name, shape, dt=F32):
            return stack.enter_context(nc.sbuf_tensor(name, shape, dt))

        def sem(name):
            return stack.enter_context(nc.semaphore(name))

        pk = sb("pk", [128, N_W])
        wqc = sb("wqc", [QR, H * QK])
        p32 = sb("p32", [KVR, 2 * H * HD + 1])
        ctxn = sb("ctxn", [CP, RING, CT, D + 1])
        ctxt = sb("ctxt", [128, RING, CT, CP])
        wup = sb("wup", [128, NCH, 128])
        wdn = sb("wdn", [128, NCH, 128])
        stats = sb("stats", [128, 3, PAIRS, 6])
        mv = sb("mv", [128, 3, PAIRS, 2])
        vpe = sb("vpe", [128, 3, PAIRS])
        rstd = sb("rstd", [128, 3, PAIRS])
        mhalf = sb("mhalf", [128, PAIRS])
        y1 = sb("y1", [128, PAIRS, 128])
        yT = sb("yT", [128, PAIRS, 128])
        qcT = sb("qcT", [QR, PAIRS, 128])
        kvt = sb("kvt", [128, PAIRS, KVR])
        kvsq = sb("kvsq", [128, PAIRS, KVR])
        kvss = sb("kvss", [128, PAIRS])
        kvms = sb("kvms", [128, PAIRS])
        kvrs = sb("kvrs", [128, PAIRS])
        kvn = sb("kvn", [128, PAIRS, KVR])
        kvnT = sb("kvnT", [KVR, PAIRS, 128])
        vv = sb("vv", [128, B, HP, 2 * VW])
        rt = [sb(f"rt{i}", [128, H, RD]) for i in range(4)]
        qtok = sb("qtok", [128, H, SLOT])
        ktok = sb("ktok", [128, H, SLOT])
        qT = sb("qT", [128, HP, 128])
        kT = sb("kT", [128, HP, 128])
        sm = sb("sm", [128, 2, HP, T])
        mx = sb("mx", [128, 2, HP])
        ss = sb("ss", [128, 2, HP, T])
        pr = sb("pr", [128, HP, 2, SLOT])
        pT = sb("pT", [128, HP, 128])
        rs = sb("rs", [128, H])
        at = sb("at", [128, H, HD])
        atT = sb("atT", [128, 128])
        x1 = sb("x1", [128, PAIRS, 128])
        y2 = sb("y2", [128, 128])
        y2T = sb("y2T", [128, 128])
        rfq = sb("rfq", [M, 128])
        rf = sb("rf", [CP, CT * M])
        kvs = sb("kvs", [M, B, D + 1])
        den = sb("den", [128, 2])
        x2 = sb("x2", [128, PAIRS, 128])
        y3 = sb("y3", [128, 128])
        y3T = sb("y3T", [128, PAIRS, 128])
        gate = sb("gate", [128, 3, PAIRS, E])
        top = sb("top", [128, PAIRS, 8])
        topi = sb("topi", [128, PAIRS, 8], U32)
        topf = sb("topf", [128, PAIRS, 2])
        tden = sb("tden", [128, 3, PAIRS])
        sel = sb("sel", [128, 5, PAIRS, E])
        cT = sb("cT", [E, PAIRS, 128])
        cb = sb("cb", [128, E, NT])
        rl = sb("rl", [128, 2, NT])
        hT = sb("hT", [128, 3, NT])
        ot = sb("ot", [128, 2, NT])
        acc = sb("acc", [128, B, SLOT])
        fin = sb("fin", [128, PAIRS, 128])

        RA = stack.enter_context(nc.psum_tensor("RA", [128, 2, 512], F32))
        RB = stack.enter_context(nc.psum_tensor("RB", [128, 2, 512], F32))
        M0 = stack.enter_context(nc.psum_tensor("M0", [128, 512], F32))
        X0 = stack.enter_context(nc.psum_tensor("X0", [128, 512], F32))
        C0 = stack.enter_context(nc.psum_tensor("C0", [128, 512], F32))
        K0 = stack.enter_context(nc.psum_tensor("K0", [128, 512], F32))

        def col(name):
            a, n = COL[name]
            return pk[:, a:a + n]

        ident = col("ident")
        xin = col("xpad").rearrange("p (q d) -> p q d", q=PAIRS)

        s_inA, s_inB, s_out = sem("s_inA"), sem("s_inB"), sem("s_out")
        s_cn = [sem(f"s_cn{i}") for i in range(RING)]
        s_ct = [sem(f"s_ct{i}") for i in range(RING)]
        s_wu, s_wd = sem("s_wu"), sem("s_wd")
        names = """pads ln_eps ln_stat ln_pow y1 yT qc kvtok kvcp kvsq kvss kvms kvpow kvn kvtp kvnT v vv
            pj rq rk qadd kadd qtp ktp qT kT sc smk smx sub prb ptp pT pv rsum atn atp atT wo x1 y2 y2tp y2T
            rfqp rfq xo den drec x2 y3 y3tp y3T cs rf ck kvs lg en one prbs topv topx topf dsum drc selc cmb
            cmtp cT cbp cb up rl h dn ot accd accp ftp fin""".split()
        S = {n: sem("s_" + n) for n in names}

        block = stack.enter_context(nc.Block())

        @block.sync
        def _(sp):
            sp.dma_start(pk[:, 0:N_A], pack128[:, 0:N_A]).then_inc(s_inA, 16)
            sp.dma_start(pk[:, N_A:N_W], pack128[:, N_A:N_W]).then_inc(s_inB, 16)
            sp.dma_start(wqc[:, :], wqcat).then_inc(s_inB, 16)
            sp.dma_start(p32[:, :], pack32).then_inc(s_inB, 16)

            def context(b):
                if b >= RING:
                    sp.wait_ge(S["cs"], b - RING + 1)
                sp.dma_start(ctxt[:, b % RING, :, :], ctx_tr[b]).then_inc(s_ct[b % RING], 16)
                if b >= RING:
                    sp.wait_ge(S["ck"], b - RING + 1)
                sp.dma_start(ctxn[:, b % RING, :, :], ctx_nat[b]).then_inc(s_cn[b % RING], 16)

            for b in range(RING):
                context(b)
            sp.dma_start(wup[:, :, :], w_up).then_inc(s_wu, 16)
            for b in range(RING, B):
                context(b)
            sp.dma_start(wdn[:, :, :], w_down).then_inc(s_wd, 16)
            sp.wait_ge(S["fin"], 2)
            sp.dma_start(out, fin[:, :, :]).then_inc(s_out, 16)
            sp.wait_ge(s_out, 16)

        @block.tensor
        def _(pe):
            def slots(a, b):
                return a[:, b // 2, (b % 2) * SLOT:(b % 2) * SLOT + SLOT]

            def ctx_scores(b):
                pe.wait_ge(s_ct[b % RING], 16 * (b // RING + 1))
                if b >= 1:
                    pe.wait_ge(S["rf"], b)
                for j in range(CT):
                    mm = pe.matmul(C0[0:CP, j * M:(j + 1) * M], ctxt[:, b % RING, j, :], col("proj"), start=True, stop=True)
                mm.then_inc(S["cs"], 1)

            def ctx_sums(b, half):
                if half == 0:
                    pe.wait_ge(S["rf"], b + 1)
                    pe.wait_ge(s_cn[b % RING], 16 * (b // RING + 1))
                    if b >= 1:
                        pe.wait_ge(S["kvs"], b)
                for j in range(half * CT // 2, (half + 1) * CT // 2):
                    mm = pe.matmul(K0[0:M, 0:D + 1], rf[:, j * M:(j + 1) * M], ctxn[:, b % RING, j, :],
                                   start=(j == 0), stop=(j == CT - 1))
                if half == 1:
                    mm.then_inc(S["ck"], 1)

            def attn_out(p):
                pe.wait_ge(S["atn"], p + 1)
                pe.transpose(M0[:, 144:272], at[:, :, :].rearrange("p h d -> p (h d)"), ident).then_inc(S["atp"], 1)
                pe.wait_ge(S["atT"], p + 1)
                pe.matmul(M0[:, 272:400], atT[:, :], col("wo"), start=True, stop=True).then_inc(S["wo"], 1)

            def y2_transpose(p):
                pe.wait_ge(S["y2"], p + 1)
                pe.transpose(X0[:, 0:128], y2[:, :], ident).then_inc(S["y2tp"], 1)

            def query_features(p):
                pe.wait_ge(S["y2T"], p + 1)
                pe.matmul(X0[0:M, 128:256], col("proj"), y2T[:, :], start=True, stop=True).then_inc(S["rfqp"], 1)

            def cross_out(p):
                pe.wait_ge(S["rfq"], p + 1)
                pe.wait_ge(S["kvs"], 2 * p + 2)
                for i in range(2):
                    mm = pe.matmul(X0[i * SLOT:(i + 1) * SLOT, 256:256 + D + 1], rfq[:, i * SLOT:(i + 1) * SLOT],
                                   kvs[:, 2 * p + i, :], start=True, stop=True)
                mm.then_inc(S["xo"], 1)

            def y3_transpose(p):
                pe.wait_ge(S["y3"], p + 1)
                pe.transpose(X0[:, 0:128], y3[:, :], ident).then_inc(S["y3tp"], 1)

            pe.wait_ge(s_inA, 16)
            for p in range(PAIRS):
                pe.wait_ge(S["y1"], p + 1)
                mm = pe.transpose(M0[:, p * 128:(p + 1) * 128], y1[:, p, :], ident)
            mm.then_inc(S["yT"], 1)
            pe.wait_ge(S["qc"], 1)
            for p in range(PAIRS):
                mm = pe.matmul(RB[:, 0, p * KVR:(p + 1) * KVR], yT[:, p, :], col("wkv"), start=True, stop=True)
            mm.then_inc(S["kvtok"], 1)
            pe.matmul(RA[0:QR, 0, :], col("wq"), yT[:, :, :].rearrange("p q t -> p (q t)"), start=True, stop=True).then_inc(S["kvtok"], 1)
            pe.wait_ge(s_inB, 48)
            ctx_scores(0)
            pe.wait_ge(S["kvn"], 1)
            for p in range(PAIRS):
                mm = pe.transpose(M0[0:KVR, p * 128:(p + 1) * 128], kvn[:, p, :], ident)
            mm.then_inc(S["kvtp"], 1)
            pe.wait_ge(S["kvnT"], 2)
            wv = p32[:, H * HD:2 * H * HD].rearrange("p (j o d) -> p j o d", j=HP, o=2)
            for b in range(B):
                for o in range(2):
                    mm = pe.matmul(RA[64 * o:64 * o + 64, 1, b * 64:(b + 1) * 64], slots(kvnT, b), wv[:, :, o, :],
                                   start=True, stop=True)
            mm.then_inc(S["v"], 1)

            for p in range(PAIRS):
                pe.wait_ge(S["vv"], 1) if p == 0 else pe.wait_ge(S["smk"], p)
                for g in range(2):
                    mm = pe.matmul(RA[:, g, 0:8 * QK], qcT[:, p, :], wqc[:, g * 8 * QK:(g + 1) * 8 * QK], start=True, stop=True)
                mm.then_inc(S["pj"], 1)
                if p >= 1:
                    pe.wait_ge(S["pT"], p)
                for g in range(2):
                    heads = RB[:, g, 0:8 * QK].rearrange("p (h d) -> p h d", h=8)
                    pe.matmul(heads[:, :, 0:HD], kvnT[:, p, :], p32[:, g * 64:(g + 1) * 64], start=True, stop=True)
                    mm = pe.matmul(heads[:, :, HD:QK], yT[:, p, :], col("krope")[:, g * 256:(g + 1) * 256], start=True, stop=True)
                mm.then_inc(S["pj"], 1)
                if p >= 1:
                    attn_out(p - 1)
                    ctx_scores(2 * p)
                pe.wait_ge(S["qadd"], p + 1)
                pe.wait_ge(S["rq"], 3 * (p + 1))
                for j in range(HP):
                    mm = pe.transpose(RA[:, j // 4, (j % 4) * 128:(j % 4 + 1) * 128],
                                      qtok[:, 2 * j:2 * j + 2, :].rearrange("p h d -> p (h d)"), ident)
                mm.then_inc(S["qtp"], 1)
                pe.wait_ge(S["kadd"], p + 1)
                for j in range(HP):
                    mm = pe.transpose(RB[:, j // 4, (j % 4) * 128:(j % 4 + 1) * 128],
                                      ktok[:, 2 * j:2 * j + 2, :].rearrange("p h d -> p (h d)"), ident)
                mm.then_inc(S["ktp"], 1)
                ctx_sums(2 * p, 0)
                if p >= 1:
                    y2_transpose(p - 1)
                pe.wait_ge(S["qT"], p + 1)
                pe.wait_ge(S["kT"], p + 1)
                for j in range(HP):
                    for i in range(2):
                        for o in range(2):
                            r = slice(64 * o, 64 * o + QK)
                            mm = pe.matmul(RA[i * SLOT:(i + 1) * SLOT, o, j * T:(j + 1) * T],
                                           qT[r, j, i * SLOT:(i + 1) * SLOT], kT[r, j, i * SLOT:i * SLOT + T],
                                           start=True, stop=True)
                mm.then_inc(S["sc"], 1)
                ctx_sums(2 * p, 1)
                if p >= 1:
                    query_features(p - 1)
                ctx_scores(2 * p + 1)
                if p >= 1:
                    cross_out(p - 1)
                pe.wait_ge(S["prb"], p + 1)
                for j in range(HP):
                    mm = pe.transpose(RB[:, j // 4, (j % 4) * 128:(j % 4 + 1) * 128],
                                      pr[:, j, :, :].rearrange("p o t -> p (o t)"), ident)
                mm.then_inc(S["ptp"], 1)
                ctx_sums(2 * p + 1, 0)
                if p >= 1:
                    y3_transpose(p - 1)
                pe.wait_ge(S["pT"], p + 1)
                if p >= 1:
                    pe.wait_ge(S["x1"], p)
                for j in range(HP):
                    for i in range(2):
                        mm = pe.matmul(M0[i * SLOT:(i + 1) * SLOT, j * 2 * VW:(j + 1) * 2 * VW],
                                       pT[:, j, i * SLOT:(i + 1) * SLOT], vv[:, 2 * p + i, j, :], start=True, stop=True)
                mm.then_inc(S["pv"], 1)
                ctx_sums(2 * p + 1, 1)
            p = PAIRS - 1
            attn_out(p)
            y2_transpose(p)
            query_features(p)
            cross_out(p)
            y3_transpose(p)

            ubank = [RA[:, 0, :], RA[:, 1, :], RB[:, 0, :]]
            obank = [RB[:, 1, :], C0[:, :]]
            pe.wait_ge(s_wu, 16)
            pe.wait_ge(S["y3T"], PAIRS)
            y3v = y3T[:, :, :].rearrange("p q (i t) -> p (q i) t", i=2)[:, :, 0:T]

            def up(c):
                if c >= 3:
                    pe.wait_ge(S["h"], c - 2)
                pe.matmul(ubank[c % 3][:, 0:NT], wup[:, c, :], y3v, start=True, stop=True).then_inc(S["up"], 1)

            def down(c):
                e, j = divmod(c, CHUNKS)
                if j == 0 and e >= 2:
                    pe.wait_ge(S["ot"], e - 1)
                if c == 0:
                    pe.wait_ge(s_wd, 16)
                pe.wait_ge(S["h"], c + 1)
                pe.matmul(obank[e % 2][:, 0:NT], wdn[:, c, :], hT[:, c % 3, :], start=(j == 0),
                          stop=(j == CHUNKS - 1)).then_inc(S["dn"], 1)

            up(0)
            up(1)
            for p in range(PAIRS):
                mm = pe.matmul(M0[:, p * E:(p + 1) * E], y3T[:, p, :], col("router"), start=True, stop=True)
            mm.then_inc(S["lg"], 1)
            up(2)
            for c in range(NCH):
                down(c)
                if c + 3 < NCH:
                    up(c + 3)
                if c == 2:
                    pe.wait_ge(S["cmb"], 1)
                    for p in range(PAIRS):
                        mm = pe.transpose(X0[0:E, p * 128:(p + 1) * 128], sel[:, 4, p, :], ident)
                    mm.then_inc(S["cmtp"], 1)
                if 3 <= c < 3 + E:
                    e = c - 3
                    if e == 0:
                        pe.wait_ge(S["cT"], 1)
                    else:
                        pe.wait_ge(S["cb"], e)
                    row = ident[0:E, e:e + 1].broadcast_to([E, 128])
                    pe.matmul(M0[:, 0:NT], row, cT[:, :, :].rearrange("p q (i t) -> p (q i) t", i=2)[:, :, 0:T],
                              start=True, stop=True).then_inc(S["cbp"], 1)
            pe.wait_ge(S["accd"], 1)
            for p in range(PAIRS):
                mm = pe.transpose(X0[:, p * 128:(p + 1) * 128], acc[:, 2 * p:2 * p + 2, :].rearrange("p b t -> p (b t)"), ident)
            mm.then_inc(S["ftp"], 1)

        @block.scalar
        def _(act):
            def copy(dst, src, after, n, done, scale=1.0):
                act.wait_ge(S[after], n)
                act.activation(dst, src, ACT.Copy, scale=scale).then_inc(S[done], 1)

            def flat(a):
                return a.rearrange("p a b -> p (a b)")

            def ctx_exp(b):
                act.wait_ge(S["cs"], b + 1)
                if b >= 1:
                    act.wait_ge(S["ck"], b)
                act.activation(rf[:, :], C0[0:CP, 0:CT * M], ACT.Exp, scale=float(D) ** -0.5).then_inc(S["rf"], 1)

            def ctx_copy(b):
                copy(kvs[:, b, :], K0[0:M, 0:D + 1], "ck", b + 1, "kvs")

            def query_exp(p):
                act.wait_ge(S["rfqp"], p + 1)
                if p >= 1:
                    act.wait_ge(S["xo"], p)
                act.activation(rfq[:, :], X0[0:M, 128:256], ACT.Exp, scale=float(D) ** -0.5).then_inc(S["rfq"], 1)

            copy(flat(yT[:, :, :]), M0[:, :], "yT", 1, "qc")
            copy(flat(qcT[:, :, :]), RA[0:QR, 0, :], "kvtok", 2, "kvnT")
            ctx_exp(0)
            act.wait_ge(s_inB, 48)
            copy(flat(kvnT[:, :, :]), M0[0:KVR, :], "kvtp", 1, "kvnT", scale=p32[:, 256:257])
            for p in range(PAIRS):
                if p >= 1:
                    copy(atT[:, :], M0[:, 144:272], "atp", p, "atT")
                    ctx_exp(2 * p)
                if p >= 1:
                    act.wait_ge(S["sc"], p)
                copy(flat(qT[:, :, :]), flat(RA[:, :, :]), "qtp", p + 1, "qT")
                copy(flat(kT[:, :, :]), flat(RB[:, :, :]), "ktp", p + 1, "kT")
                if p >= 1:
                    copy(y2T[:, :], X0[:, 0:128], "y2tp", p, "y2T")
                ctx_copy(2 * p)
                if p >= 1:
                    query_exp(p - 1)
                act.wait_ge(S["pads"], 1)
                act.wait_ge(S["sub"], p + 1)
                if p >= 1:
                    act.wait_ge(S["ptp"], p)
                act.activation(pr[:, :, :, 0:T].rearrange("p j o t -> p o j t"), ss[:, :, :, :], ACT.Exp,
                               scale=float(QK) ** -0.5).then_inc(S["prb"], 1)
                ctx_exp(2 * p + 1)
                if p >= 1:
                    act.wait_ge(S["pv"], p)
                copy(flat(pT[:, :, :]), flat(RB[:, :, :]), "ptp", p + 1, "pT")
                if p >= 1:
                    copy(y3T[:, p - 1, :], X0[:, 0:128], "y3tp", p, "y3T")
                ctx_copy(2 * p + 1)
            p = PAIRS - 1
            copy(atT[:, :], M0[:, 144:272], "atp", p + 1, "atT")
            copy(y2T[:, :], X0[:, 0:128], "y2tp", p + 1, "y2T")
            query_exp(p)
            copy(y3T[:, p, :], X0[:, 0:128], "y3tp", p + 1, "y3T")

            ubank = [RA[:, 0, :], RA[:, 1, :], RB[:, 0, :]]

            def relu(c):
                act.wait_ge(S["up"], c + 1)
                if c >= 2:
                    act.wait_ge(S["h"], c - 1)
                act.activation(rl[:, c % 2, :], ubank[c % 3][:, 0:NT], ACT.Relu).then_inc(S["rl"], 1)

            relu(0)
            relu(1)
            act.wait_ge(S["lg"], 1)
            act.activation(gate[:, 0, :, :], M0[:, 0:PAIRS * E].rearrange("p (q e) -> p q e", q=PAIRS), ACT.Exp,
                           scale=-1.0).then_inc(S["en"], 1)
            for c in range(2, NCH):
                relu(c)
                if c == 5:
                    copy(flat(cT[:, :, :]), X0[0:E, :], "cmtp", 1, "cT")
                if 6 <= c < 6 + E:
                    e = c - 6
                    copy(cb[:, e, :], M0[:, 0:NT], "cbp", e + 1, "cb")

        @block.gpsimd
        def _(pool):
            pool.memset(mhalf[:, :], -0.5)
            pool.memset(vv[:, :, :, :], 0.0)
            pool.memset(qtok[:, :, QK:SLOT], 0.0)
            pool.memset(ktok[:, :, QK:SLOT], 0.0)
            pool.memset(pr[:, :, :, T:SLOT], 0.0)
            pool.memset(acc[:, :, :], 0.0).then_inc(S["pads"], 1)

            def power(dst, src, after, n, done):
                pool.wait_ge(S[after], n)
                pool.tensor_tensor(dst, src, mhalf[:, 0:src.shape[1]], ALU.pow).then_inc(S[done], 1)

            pool.wait_ge(S["pads"], 1)
            power(rstd[:, 0, :], vpe[:, 0, :], "ln_eps", 1, "ln_pow")
            power(kvrs[:, :], kvms[:, :], "kvms", 1, "kvpow")
            n = 1
            for p in range(PAIRS):
                if p >= 1:
                    n += 1
                    power(rstd[:, 1, p - 1:p], vpe[:, 1, p - 1:p], "ln_eps", n, "ln_pow")
                    n += 1
                    power(rstd[:, 2, p - 1:p], vpe[:, 2, p - 1:p], "ln_eps", n, "ln_pow")
            for k in (1, 2):
                n += 1
                power(rstd[:, k, 3:4], vpe[:, k, 3:4], "ln_eps", n, "ln_pow")

        @block.vector
        def _(v):
            count = {}

            def step(ins, name):
                ins.then_inc(S[name], 1)
                count[name] = count.get(name, 0) + 1

            def own(name):
                v.wait_ge(S[name], count[name])

            def bcast(a, shape):
                return a.unsqueeze(len(a.shape)).broadcast_to(shape)

            def ln_stats(x, k, p):
                step(v.bn_stats(stats[:, k, p, :], x), "ln_stat")
                own("ln_stat")
                step(v.bn_aggr(mv[:, k, p, :], stats[:, k, p, :]), "ln_stat")

            def ln_eps(k, p0, p1):
                own("ln_stat")
                step(v.tensor_scalar(vpe[:, k, p0:p1], mv[:, k, p0:p1, 1], LN_EPS, None, ALU.add), "ln_eps")

            def ln_apply(dst, x, k, p):
                return v.tensor_scalar(dst, x, mv[:, k, p, 0:1], rstd[:, k, p:p + 1], ALU.subtract, ALU.mult)

            v.wait_ge(s_inA, 16)
            for p in range(PAIRS):
                ln_stats(xin[:, p, :], 0, p)
            ln_eps(0, 0, PAIRS)
            v.wait_ge(S["ln_pow"], 1)
            for p in range(PAIRS):
                step(ln_apply(y1[:, p, :], xin[:, p, :], 0, p), "y1")
            v.wait_ge(S["kvtok"], 1)
            step(v.tensor_copy(kvt[:, :, :].rearrange("p a b -> p (a b)"), RB[:, 0, 0:PAIRS * KVR]), "kvcp")
            own("kvcp")
            step(v.tensor_tensor(kvsq[:, :, :], kvt[:, :, :], kvt[:, :, :], ALU.mult), "kvsq")
            own("kvsq")
            step(v.tensor_reduce(kvss[:, :], kvsq[:, :, :], AX_X, ALU.add), "kvss")
            own("kvss")
            step(v.tensor_scalar(kvms[:, :], kvss[:, :], 1.0 / KVR, RMS_EPS, ALU.mult, ALU.add), "kvms")
            v.wait_ge(S["kvpow"], 1)
            step(v.tensor_tensor(kvn[:, :, :], kvt[:, :, :], bcast(kvrs[:, :], [128, PAIRS, KVR]), ALU.mult), "kvn")
            v.wait_ge(S["pads"], 1)
            v.memset(vv[0:64, :, :, HD:HD + 1], 1.0)
            v.memset(vv[64:128, :, :, VW + HD:VW + HD + 1], 1.0)
            v.wait_ge(S["v"], 1)
            for o in range(2):
                src = RA[64 * o:64 * o + 64, 1, :].rearrange("p (b j d) -> p b j d", b=B, j=HP)
                ins = v.tensor_copy(vv[64 * o:64 * o + 64, :, :, o * VW:o * VW + HD], src)
            step(ins, "vv")

            def heads(region):
                return region[:, :, 0:8 * QK].rearrange("p g (h d) -> p g h d", h=8)

            def rotate(region, tok, t1, t2, done, n):
                src = heads(region)
                th = tok[:, :, :].rearrange("p (g h) d -> p g h d", g=2)
                c4 = [128, 2, 8, RD]
                half = [128, 2, 8, RD // 2]

                def table(name, a, b, shape):
                    return col(name)[:, a:b].unsqueeze(1).unsqueeze(1).broadcast_to(shape)

                v.wait_ge(S["pj"], n)
                r1 = t1[:, :, :].rearrange("p (g h) d -> p g h d", g=2)
                r2 = t2[:, :, :].rearrange("p (g h) d -> p g h d", g=2)
                v.tensor_tensor(r1, src[:, :, :, HD:QK], table("cos", 0, RD, c4), ALU.mult)
                step(v.tensor_tensor(r2[:, :, :, 0:16], src[:, :, :, HD + 16:QK], table("sin", 0, 16, half), ALU.mult), done)
                step(v.tensor_tensor(r2[:, :, :, 16:32], src[:, :, :, HD:HD + 16], table("sin", 16, 32, half), ALU.mult), done)
                step(v.tensor_copy(th[:, :, :, 0:HD], src[:, :, :, 0:HD]), done)

            def attn_norm(p):
                v.wait_ge(S["pv"], p + 1)
                a = M0[:, 0:HP * 2 * VW].rearrange("p (h d) -> p h d", h=H)
                step(v.reciprocal(rs[:, :], a[:, :, HD]), "rsum")
                own("rsum")
                if p >= 1:
                    v.wait_ge(S["atp"], p)
                step(v.tensor_tensor(at[:, :, :], a[:, :, 0:HD], bcast(rs[:, :], [128, H, HD]), ALU.mult), "atn")

            def residual1(p):
                v.wait_ge(S["wo"], p + 1)
                step(v.tensor_tensor(x1[:, p, :], M0[:, 272:400], xin[:, p, :], ALU.add), "x1")
                own("x1")
                ln_stats(x1[:, p, :], 1, p)
                ln_eps(1, p, p + 1)

            def norm2(p):
                v.wait_ge(S["ln_pow"], 2 * p + 2)
                if p >= 1:
                    v.wait_ge(S["y2tp"], p)
                step(ln_apply(y2[:, :], x1[:, p, :], 1, p), "y2")

            def residual2(p):
                v.wait_ge(S["xo"], p + 1)
                step(v.tensor_scalar(den[:, 0:1], X0[:, 256 + D:257 + D], XN_EPS * float(M) ** 0.5, None, ALU.add), "den")
                own("den")
                step(v.reciprocal(den[:, 1:2], den[:, 0:1]), "drec")
                own("drec")
                step(v.scalar_tensor_tensor(out=x2[:, p, :], in0=X0[:, 256:256 + D], scalar=den[:, 1:2], in1=x1[:, p, :],
                                            op0=ALU.mult, op1=ALU.add), "x2")
                own("x2")
                ln_stats(x2[:, p, :], 2, p)
                ln_eps(2, p, p + 1)

            def norm3(p):
                v.wait_ge(S["ln_pow"], 2 * p + 3)
                if p >= 1:
                    v.wait_ge(S["y3tp"], p)
                step(ln_apply(y3[:, :], x2[:, p, :], 2, p), "y3")

            v.wait_ge(s_inB, 48)
            for p in range(PAIRS):
                if p >= 1:
                    attn_norm(p - 1)
                    v.wait_ge(S["ktp"], p)
                rotate(RA, qtok, rt[0], rt[1], "rq", 2 * p + 1)
                own("rq")
                step(v.tensor_tensor(qtok[:, :, HD:QK], rt[0][:, :, :], rt[1][:, :, :], ALU.add), "qadd")
                rotate(RB, ktok, rt[2], rt[3], "rk", 2 * p + 2)
                own("rk")
                step(v.tensor_tensor(ktok[:, :, HD:QK], rt[2][:, :, :], rt[3][:, :, :], ALU.add), "kadd")
                if p >= 1:
                    residual1(p - 1)
                    norm2(p - 1)
                v.wait_ge(S["sc"], p + 1)
                maskb = col("mask").unsqueeze(1).unsqueeze(1).broadcast_to([128, 2, HP, T])
                if p >= 1:
                    own("sub")
                step(v.tensor_tensor(sm[:, :, :, :], RA[:, :, 0:HP * T].rearrange("p o (j t) -> p o j t", j=HP), maskb, ALU.add), "smk")
                own("smk")
                step(v.tensor_reduce(mx[:, :, :], sm[:, :, :, :], AX_X, ALU.max), "smx")
                own("smx")
                if p >= 1:
                    v.wait_ge(S["prb"], p)
                step(v.tensor_tensor(ss[:, :, :, :], sm[:, :, :, :], bcast(mx[:, :, :], [128, 2, HP, T]), ALU.subtract), "sub")
                if p >= 1:
                    residual2(p - 1)
                    norm3(p - 1)
            p = PAIRS - 1
            attn_norm(p)
            residual1(p)
            norm2(p)
            residual2(p)
            norm3(p)

            ubank = [RA[:, 0, :], RA[:, 1, :], RB[:, 0, :]]
            obank = [RB[:, 1, :], C0[:, :]]

            def hidden(c):
                v.wait_ge(S["rl"], c + 1)
                if c >= 3:
                    v.wait_ge(S["dn"], c - 2)
                step(v.scalar_tensor_tensor(out=hT[:, c % 3, :], in0=ubank[c % 3][:, 0:NT], scalar=0.0, in1=rl[:, c % 2, :],
                                            op0=ALU.max, op1=ALU.mult), "h")

            accv = acc[:, :, 0:T]

            def tok(a):
                return a.rearrange("p (b t) -> p b t", b=B)

            def expert_out(e):
                v.wait_ge(S["dn"], CHUNKS * (e + 1))
                if e == 0:
                    step(v.tensor_copy(accv, tok(obank[0][:, 0:NT])), "ot")
                    return
                v.wait_ge(S["cb"], e)
                if e >= 2:
                    own("accp")
                step(v.tensor_tensor(ot[:, 0, :], obank[e % 2][:, 0:NT], cb[:, e - 1, :], ALU.mult), "ot")
                own("ot")
                step(v.tensor_tensor(accv, accv, tok(ot[:, 0, :]), ALU.add), "accd" if e == E else "accp")

            def choose():
                shape = [128, PAIRS, E]
                v.wait_ge(S["en"], 1)
                step(v.tensor_scalar(gate[:, 1, :, :], gate[:, 0, :, :], 1.0, None, ALU.add), "one")
                own("one")
                step(v.reciprocal(gate[:, 2, :, :], gate[:, 1, :, :]), "prbs")
                own("prbs")
                for p in range(PAIRS):
                    step(v.max(top[:, p, :], gate[:, 2, p, :]), "topv")
                own("topv")
                for p in range(PAIRS):
                    step(v.max_index(topi[:, p, :], top[:, p, :], gate[:, 2, p, :]), "topx")
                own("topx")
                step(v.tensor_copy(topf[:, :, :], topi[:, :, 0:2]), "topf")
                step(v.tensor_tensor(tden[:, 0, :], top[:, :, 0], top[:, :, 1], ALU.add), "dsum")
                own("dsum")
                step(v.tensor_scalar(tden[:, 1, :], tden[:, 0, :], TOPK_EPS, None, ALU.add), "dsum")
                own("dsum")
                step(v.reciprocal(tden[:, 2, :], tden[:, 1, :]), "drc")
                own("topf")
                iota = col("iota").unsqueeze(1).broadcast_to(shape)
                for k in range(2):
                    step(v.tensor_tensor(sel[:, k, :, :], iota, bcast(topf[:, :, k], shape), ALU.is_equal), "selc")
                own("selc")
                for k in range(2):
                    step(v.tensor_tensor(sel[:, 2 + k, :, :], sel[:, k, :, :], bcast(top[:, :, k], shape), ALU.mult), "selc")
                own("selc")
                step(v.tensor_tensor(sel[:, 0, :, :], sel[:, 2, :, :], sel[:, 3, :, :], ALU.add), "selc")
                own("selc")
                own("drc")
                step(v.tensor_tensor(sel[:, 4, :, :], sel[:, 0, :, :], bcast(tden[:, 2, :], shape), ALU.mult), "cmb")

            for c in range(NCH):
                hidden(c)
                if c == 1:
                    choose()
                if c % CHUNKS == 1 and c > CHUNKS:
                    expert_out(c // CHUNKS - 1)
            expert_out(E)
            v.wait_ge(S["ftp"], 1)
            step(v.tensor_tensor(fin[:, 0:2, :], X0[:, 0:256].rearrange("p (q d) -> p q d", q=2), x2[:, 0:2, :], ALU.add), "fin")
            step(v.tensor_tensor(fin[:, 2:4, :], X0[:, 256:512].rearrange("p (q d) -> p q d", q=2), x2[:, 2:4, :], ALU.add), "fin")


def _constants():
    mask = np.zeros((2, SLOT, T), np.float32)
    mask[:, :T] = np.where(np.tril(np.ones((T, T), bool)), 0.0, NEG)
    inv_freq = 1.0 / 10000.0 ** (np.arange(0, RD, 2, dtype=np.float32) / RD)
    freqs = np.outer(np.arange(T, dtype=np.float32), inv_freq)
    cos, sin = np.zeros((2, SLOT, RD), np.float32), np.zeros((2, SLOT, RD), np.float32)
    cos[:, :T] = np.cos(np.concatenate([freqs, freqs], -1))
    sin[:, :T] = np.sin(np.concatenate([-freqs, freqs], -1))
    return {
        "ident": np.eye(128, dtype=np.float32), "mask": mask.reshape(128, T), "cos": cos.reshape(128, RD),
        "sin": sin.reshape(128, RD), "iota": np.tile(np.arange(E, dtype=np.float32), (128, 1)),
    }


def kernel(x, ctx_1024, L0_attn_W_kv, L0_attn_g_kv, L0_attn_W_kdec, L0_attn_W_vdec, L0_attn_W_q, L0_attn_W_qdec,
           L0_attn_W_krope, L0_attn_W_qrope, L0_attn_W_o, L0_xattn_projection, L0_ffn_W_router, L0_ffn_W_up,
           L0_ffn_W_down, L0_ffn_W_sh_up, L0_ffn_W_sh_down):
    import concourse.bacc as _bacc
    from concourse.bass_utils import run_bass_kernel_spmd as _run

    a = {k: np.asarray(v) for k, v in locals().items() if k[0] != "_"}
    xp = np.zeros((PAIRS, 2, SLOT, D), np.float32)
    xp[:, :, :T] = a["x"].reshape(PAIRS, 2, T, D)
    parts = _constants() | {
        "xpad": xp.reshape(PAIRS, 128, D).transpose(1, 0, 2).reshape(128, PAIRS * D),
        "wkv": a["L0_attn_W_kv"], "wq": a["L0_attn_W_q"], "krope": a["L0_attn_W_krope"], "wo": a["L0_attn_W_o"],
        "proj": a["L0_xattn_projection"].T, "router": a["L0_ffn_W_router"],
    }
    pack128 = np.concatenate([parts[k] for k in W128], 1)
    wqcat = np.concatenate([a["L0_attn_W_qdec"].reshape(QR, H, HD), a["L0_attn_W_qrope"].reshape(QR, H, RD)], 2)
    pack32 = np.concatenate([a["L0_attn_W_kdec"], a["L0_attn_W_vdec"], a["L0_attn_g_kv"].reshape(KVR, 1)], 1)
    c = a["ctx_1024"].reshape(B, CP, CT, D)
    ctx_nat = np.concatenate([c, np.ones((B, CP, CT, 1), np.float32)], 3)
    ctx_tr = c.transpose(0, 3, 2, 1)
    up = np.concatenate([a["L0_ffn_W_sh_up"][None], a["L0_ffn_W_up"]], 0).reshape(E + 1, D, CHUNKS, 128)
    down = np.concatenate([a["L0_ffn_W_sh_down"][None], a["L0_ffn_W_down"]], 0).reshape(NCH, 128, D)
    arrays = {
        "pack128": pack128, "wqcat": wqcat.reshape(QR, H * QK), "pack32": pack32, "ctx_nat": ctx_nat, "ctx_tr": ctx_tr,
        "w_up": up.transpose(1, 0, 2, 3).reshape(D, NCH, 128), "w_down": down.transpose(1, 0, 2),
    }
    arrays = {k: np.ascontiguousarray(v) for k, v in arrays.items()}
    nc = _bacc.Bacc("TRN2", target_bir_lowering=False, num_devices=1)
    args = [nc.dram_tensor(k, v.shape, mybir.dt.from_np(v.dtype), kind="ExternalInput").ap() for k, v in arrays.items()]
    out = nc.dram_tensor("out", (128, PAIRS, D), F32, kind="ExternalOutput").ap()
    decoder_layer(nc, *args, out)
    got = _run(nc, [arrays], core_ids=[0]).results[0]["out"]
    return got.reshape(2, SLOT, PAIRS, D).transpose(2, 0, 1, 3)[:, :, :T].reshape(B, T, D)
```

```python
from contextlib import ExitStack

import concourse.bass as bass
from concourse import mybir
import numpy as np

F32 = mybir.dt.float32
F32R = mybir.dt.float32r
U32 = mybir.dt.uint32
ALU = mybir.AluOpType
ACT = mybir.ActivationFunctionType
AX_X = mybir.AxisListType.X

B, T, D = 8, 56, 128
H, HD, RD = 16, 8, 32
KVR, QR = 32, 64
L, M = 1500, 32
E, HID = 8, 512
LN_EPS, RMS_EPS, XN_EPS, TOPK_EPS = 1e-5, 1e-6, 1e-6, 1e-6

SLOT = 64
PAIRS = B // 2
QK = HD + RD
HP = H // 2
VW = HD + 1
NT = B * T
GR = 4
CT = -(-L // 128)
GL = CT * 32
CW = D + 2
RING = 2
CHUNKS = HID // 128
NCH = (E + 1) * CHUNKS
PIECE = 6
NPC = NCH // PIECE
PPP = 2 * NPC // PAIRS
LATE = 3
LATE_AT = (3, 11, 19)
WARM = 3
WARM_RFQ, WARM_Y3, WARM_Y3T = 2, 10, 3
NEG = -3.0e38

W128 = dict(ident=128, xpad=PAIRS * 128, wkv=KVR, wq=QR, proj=M, krope=H * RD, wo=D, router=E, mask=T, cos=RD, sin=RD, iota=E)
COL = {}
for _k, _n in W128.items():
    COL[_k] = (sum(v for v in list(W128.values())[:len(COL)]), _n)
N_X = sum(W128[k] for k in ("ident", "xpad"))
N_A = N_X + sum(W128[k] for k in ("wkv", "wq", "proj"))
N_W = sum(W128.values())


def decoder_layer(nc, pack128, wqcat, pack32, ctx_nat, ctx_tr, w_up, w_down, share, out):
    with ExitStack() as stack:
        def sb(name, shape, dt=F32):
            return stack.enter_context(nc.sbuf_tensor(name, shape, dt))

        def sem(name):
            return stack.enter_context(nc.semaphore(name))

        pk = sb("pk", [128, N_W])
        identr = sb("identr", [128, 128], F32R)
        maskr = sb("maskr", [128, T], F32R)
        wqc = sb("wqc", [QR, H * QK])
        p32 = sb("p32", [KVR, 2 * H * HD + 1])
        ctxs = sb("ctxs", [128, 2 * CT * 2 * CW], F32R)
        craw = sb("craw", [128, RING * (GR * GL + CT * CW)])
        wraw = sb("wraw", [128, 2, PIECE, 128])
        wuh, wul = sb("wuh", [128, NCH, 128], F32R), sb("wul", [128, NCH, 128], F32R)
        wdh, wdl = sb("wdh", [128, NCH, 128], F32R), sb("wdl", [128, NCH, 128], F32R)
        stats = sb("stats", [128, 3, PAIRS, 6])
        mv = sb("mv", [128, 3, PAIRS, 2])
        vpe = sb("vpe", [128, 3, PAIRS])
        rstd = sb("rstd", [128, 3, PAIRS])
        mhalf = sb("mhalf", [128, PAIRS])
        y1 = sb("y1", [128, PAIRS, 128])
        yT = sb("yT", [128, PAIRS, 128])
        qcT = sb("qcT", [QR, PAIRS, 128])
        kvss = sb("kvss", [128, PAIRS])
        kvms = sb("kvms", [128, PAIRS])
        kvrs = sb("kvrs", [128, PAIRS])
        kvnT = sb("kvnT", [KVR, PAIRS, 128])
        vv = sb("vv", [128, B, HP, 2 * VW])
        rt = [sb(f"rt{i}", [128, H, RD]) for i in range(2)]
        qtok = sb("qtok", [128, H, SLOT])
        ktok = sb("ktok", [128, H, SLOT])
        qT = sb("qT", [128, HP, 128])
        kT = sb("kT", [128, HP, 128])
        sm = sb("sm", [128, 2, HP, T])
        mx = sb("mx", [128, 2, HP])
        pr = sb("pr", [128, HP, 2, SLOT])
        pT = sb("pT", [128, HP, 128])
        rs = sb("rs", [128, H])
        at = sb("at", [128, H, HD])
        atT = sb("atT", [128, 128])
        x1 = sb("x1", [128, PAIRS, 128])
        y2 = sb("y2", [128, 128])
        y2T = sb("y2T", [128, 128])
        rfq = sb("rfq", [M, 128])
        rf = sb("rf", [128, GL])
        rft = sb("rft", [128, CT, M])
        rfs = sb("rfs", [128, CT, 2, M], F32R)
        kvlh = sb("kvlh", [2 * M, 2 * CW])
        kvs = sb("kvs", [M, B, D + 1])
        den = sb("den", [128, 2])
        x2 = sb("x2", [128, PAIRS, 128])
        y3 = sb("y3", [128, 128])
        y3T = sb("y3T", [128, PAIRS, 128])
        y3h, y3l = sb("y3h", [128, PAIRS, 128], F32R), sb("y3l", [128, PAIRS, 128], F32R)
        gate = sb("gate", [128, 3, PAIRS, E])
        top = sb("top", [128, PAIRS, 8])
        topi = sb("topi", [128, PAIRS, 8], U32)
        topf = sb("topf", [128, PAIRS, 2])
        tden = sb("tden", [128, 3, PAIRS])
        sel = sb("sel", [128, 5, PAIRS, E])

        RA = stack.enter_context(nc.psum_tensor("RA", [128, 2, 512], F32))
        RB = stack.enter_context(nc.psum_tensor("RB", [128, 2, 512], F32))
        M0 = stack.enter_context(nc.psum_tensor("M0", [128, 512], F32))
        X0 = stack.enter_context(nc.psum_tensor("X0", [128, 512], F32))
        C0 = stack.enter_context(nc.psum_tensor("C0", [128, 512], F32))
        K0 = stack.enter_context(nc.psum_tensor("K0", [128, 512], F32))

        cb = craw[:, 0:E * NT].rearrange("p (e t) -> p e t", e=E)
        hf = craw[:, E * NT:(E + 4) * NT].rearrange("p (k t) -> p k t", k=4)
        hh, hl = (ctxs[:, k * 4 * NT:(k + 1) * 4 * NT].rearrange("p (k t) -> p k t", k=4) for k in range(2))
        rl = [a[:, :, :].rearrange("p h d -> p (h d)")[:, 0:NT] for a in rt]
        ot = qT[:, :, :].rearrange("p j t -> p (j t)")[:, 0:2 * NT].rearrange("p (k t) -> p k t", k=2)
        cT = kT[0:E, 0:4, :]
        acc = kT[:, 4:8, :].rearrange("p q (i t) -> p (q i) t", i=2)
        accv = acc[:, :, 0:T]
        fin = y1
        kvt, kvsq, kvn = (x1[:, k, :].rearrange("p (q d) -> p q d", q=PAIRS) for k in range(3))
        kvl, kvh = kvlh[0:M, :], kvlh[M:2 * M, :]
        ctxn = craw[:, RING * GR * GL:].rearrange("p (r d) -> p r d", r=RING)
        ctxtv = craw[:, 0:RING * GR * GL].rearrange("p (r g t) -> p r g t", r=RING, g=GR)
        ctxsv = ctxs[:, :].rearrange("p (r j k d) -> p r j k d", r=2, j=CT, k=2)
        ubank = [RA[:, 0, :], RA[:, 1, :], RB[:, 0, :], RB[:, 1, :]]
        obank = [C0[:, :], K0[:, :]]
        fbank = [a[:, 0:256].rearrange("p (q d) -> p q d", q=2) for a in (X0, M0)]

        def on_pool(c):
            return c % 8 in (1, 3, 7) and c < NCH - CHUNKS

        def low_count(c):
            return sum(on_pool(k) == on_pool(c) for k in range(c + 1))

        def wait_low(engine, c):
            engine.wait_ge(S["hlp"] if on_pool(c) else S["hlv"], low_count(c))

        def tiles(b):
            return ctxn[:, b % RING, :].rearrange("p (j d) -> p j d", j=CT)

        def col(name):
            a, n = COL[name]
            return pk[:, a:a + n]

        ident = col("ident")
        xin = col("xpad").rearrange("p (q d) -> p q d", q=PAIRS)

        s_x, s_inA, s_inB, s_out = sem("s_x"), sem("s_inA"), sem("s_inB"), sem("s_out")
        s_share = sem("s_share")
        s_cb = [sem("s_cb0"), sem("s_cb1")]
        s_cn = [sem(f"s_cn{i}") for i in range(RING)]
        s_ct = [sem(f"s_ct{i}") for i in range(RING)]
        s_w = [sem("s_w0"), sem("s_w1")]
        names = """pads ln_eps ln_stat ln_pow y1 yT qc kvtok kvcp kvsq kvss kvms kvpow kvn kvtp kvnT v vv
            pq pk rq rk qadd kadd qtp ktp qT kT sc idm smx sub prb ptp pT pv rsum atn atp atT wo x1 y2 y2tp y2T
            rfqp rfq xo den drec x2 y3 y3tp y3T y3l cs rf rft fh rfs ch cl ck kvl kvh kvs wh wl lg en one prbs topv topx topf dsum drc selc cmb
            cmtp cT up rl h hh hlv hlp dn ot acc0 acc7 accd accp ftp fin""".split()
        S = {n: sem("s_" + n) for n in names}

        block = stack.enter_context(nc.Block())

        @block.sync
        def _(sp):
            sp.dma_start(pk[:, 0:N_X], pack128[:, 0:N_X]).then_inc(s_x, 16)
            sp.dma_start(pk[:, N_X:N_A], pack128[:, N_X:N_A]).then_inc(s_inA, 16)

            def context_t(b):
                if b >= RING:
                    sp.wait_ge(S["cs"], b - RING + 1)
                sp.dma_start(ctxtv[:, b % RING, :, :], ctx_tr[b]).then_inc(s_ct[b % RING], 16)

            def context_n(b):
                if b >= RING:
                    sp.wait_ge(S["cl"], b - RING + 1)
                sp.dma_start(ctxn[:, b % RING, :], ctx_nat[b]).then_inc(s_cn[b % RING], 16)

            def weights(k):
                if k >= 2:
                    sp.wait_ge(S["wl"], k - 1)
                src = w_up if k < NPC else w_down
                j = k % NPC
                sp.dma_start(wraw[:, k % 2, :, :], src[:, j * PIECE:(j + 1) * PIECE, :]).then_inc(s_w[k % 2], 16)

            context_t(0)
            sp.dma_start(pk[:, N_A:N_W], pack128[:, N_A:N_W]).then_inc(s_inB, 16)
            sp.dma_start(wqc[:, :], wqcat).then_inc(s_inB, 16)
            sp.dma_start(p32[:, :], pack32).then_inc(s_inB, 16)
            context_n(0)
            k = 0
            for b in range(1, B):
                context_t(b)
                context_n(b)
                for _ in range((0, 2, 0, 2, 1, 2, 1, 3)[b]):
                    weights(k)
                    k += 1
            assert k == 2 * NPC - 1
            sp.wait_ge(S["cT"], 1)
            sp.dma_start(share, cT[:, :, :].rearrange("p q (i t) -> p (q i) t", i=2)[:, :, 0:T]).then_inc(s_share, 16)
            sp.wait_ge(s_share, 16)
            for e in range(E):
                sp.dma_start(cb[:, e, :], share[e:e + 1, :, :].rearrange("e b t -> e (b t)").broadcast_to([128, NT])).then_inc(s_cb[e > 1], 16)
            weights(k)
            for k in range(2):
                sp.wait_ge(S["fin"], k + 1)
                sp.dma_start(out[:, 2 * k:2 * k + 2, :], fin[:, 2 * k:2 * k + 2, :]).then_inc(s_out, 16)
            sp.wait_ge(s_out, 32)

        @block.tensor
        def _(pe):
            def slots(a, b):
                return a[:, b // 2, (b % 2) * SLOT:(b % 2) * SLOT + SLOT]

            def ctx_scores(b):
                pe.wait_ge(s_ct[b % RING], 16 * (b // RING + 1))
                if b >= 1:
                    pe.wait_ge(S["rf"], b)
                for g in range(GR):
                    mm = pe.matmul(C0[M * g:M * (g + 1), 0:GL], col("proj"), ctxtv[:, b % RING, g, :], start=True, stop=True)
                mm.then_inc(S["cs"], 1)

            def ctx_sums(b, half):
                if half == 0:
                    pe.wait_ge(S["rfs"], b + 1)
                    pe.wait_ge(S["cl"], b + 1)
                    if b >= 1:
                        pe.wait_ge(S["kvs"], b)
                for j in range(half * CT // 2, (half + 1) * CT // 2):
                    mm = pe.matmul(K0[0:2 * M, 0:2 * CW], rfs[:, j, :, :].rearrange("p k m -> p (k m)"),
                                   ctxsv[:, b % 2, j, :, :].rearrange("p k d -> p (k d)"), start=(j == 0), stop=(j == CT - 1))
                if half == 1:
                    mm.then_inc(S["ck"], 1)

            def queries(p):
                if p >= 1:
                    pe.wait_ge(S["sub"], 2 * p)
                for g in range(2):
                    mm = pe.matmul(RA[:, g, 0:8 * QK], qcT[:, p, :], wqc[:, g * 8 * QK:(g + 1) * 8 * QK], start=True, stop=True)
                mm.then_inc(S["pq"], 1)

            def key_heads(g):
                return RB[:, g, 0:8 * QK].rearrange("p (h d) -> p h d", h=8)

            def queries_turned(p):
                pe.wait_ge(S["qadd"], p + 1)
                pe.wait_ge(S["rq"], 3 * (p + 1))
                for j in range(HP):
                    mm = pe.transpose(RA[:, j // 4, (j % 4) * 128:(j % 4 + 1) * 128],
                                      qtok[:, 2 * j:2 * j + 2, :].rearrange("p h d -> p (h d)"), ident)
                mm.then_inc(S["qtp"], 1)

            def rope_keys(p):
                if p >= 1:
                    pe.wait_ge(S["pT"], 2 * p)
                for g in range(2):
                    pe.matmul(key_heads(g)[:, :, HD:QK], yT[:, p, :], col("krope")[:, g * 256:(g + 1) * 256], start=True, stop=True)

            def content_keys(p):
                for g in range(2):
                    mm = pe.matmul(key_heads(g)[:, :, 0:HD], kvnT[:, p, :], p32[:, g * 64:(g + 1) * 64], start=True, stop=True)
                mm.then_inc(S["pk"], 1)

            def heads_turned(p):
                pe.wait_ge(S["atn"], p + 1)
                pe.transpose(M0[:, 144:272], at[:, :, :].rearrange("p h d -> p (h d)"), ident).then_inc(S["atp"], 1)

            def attn_out(p):
                pe.wait_ge(S["atT"], p + 1)
                pe.matmul(M0[:, 272:400], atT[:, :], col("wo"), start=True, stop=True).then_inc(S["wo"], 1)

            def y2_transpose(p):
                pe.wait_ge(S["y2"], p + 1)
                if p >= 1:
                    pe.wait_ge(S["y3T"], 2 * p)
                pe.transpose(X0[:, 0:128], y2[:, :], ident).then_inc(S["y2tp"], 1)

            def query_features(p):
                pe.wait_ge(S["y2T"], p + 1)
                pe.matmul(X0[0:M, 128:256], col("proj"), y2T[:, :], start=True, stop=True).then_inc(S["rfqp"], 1)

            def cross_out(p):
                pe.wait_ge(S["rfq"], p + 1)
                pe.wait_ge(S["kvs"], 2 * p + 2)
                for i in range(2):
                    mm = pe.matmul(X0[i * SLOT:(i + 1) * SLOT, 256:256 + D + 1], rfq[:, i * SLOT:(i + 1) * SLOT],
                                   kvs[:, 2 * p + i, :], start=True, stop=True)
                mm.then_inc(S["xo"], 1)

            def y3_transpose(p):
                pe.wait_ge(S["y3"], p + 1)
                pe.transpose(X0[:, 0:128], y3[:, :], ident).then_inc(S["y3tp"], 1)

            pe.wait_ge(S["pads"], 1)
            for _ in range(WARM):
                pe.matmul(K0[:, :], vv[:, 0:2, :, :].rearrange("p b j d -> p (b j d)")[:, 0:128],
                          vv[:, :, :, :].rearrange("p b j d -> p (b j d)")[:, 0:512], start=True, stop=True)
            for p in range(PAIRS):
                pe.wait_ge(S["y1"], p + 1)
                mm = pe.transpose(M0[:, p * 128:(p + 1) * 128], y1[:, p, :], ident)
            mm.then_inc(S["yT"], 1)
            pe.wait_ge(s_inA, 16)
            ctx_scores(0)
            pe.wait_ge(S["qc"], 1)
            for p in range(PAIRS):
                mm = pe.matmul(X0[:, p * KVR:(p + 1) * KVR], yT[:, p, :], col("wkv"), start=True, stop=True)
            mm.then_inc(S["kvtok"], 1)
            pe.matmul(RA[0:QR, 0, :], col("wq"), yT[:, :, :].rearrange("p q t -> p (q t)"), start=True, stop=True).then_inc(S["kvtok"], 1)
            pe.wait_ge(s_inB, 48)
            pe.wait_ge(S["kvnT"], 1)
            queries(0)
            rope_keys(0)
            pe.wait_ge(S["kvn"], 1)
            for p in range(PAIRS):
                mm = pe.transpose(M0[0:KVR, p * 128:(p + 1) * 128], kvn[:, p, :], ident)
            mm.then_inc(S["kvtp"], 1)
            pe.wait_ge(S["kvnT"], 2)
            content_keys(0)
            wv = p32[:, H * HD:2 * H * HD].rearrange("p (j o d) -> p j o d", j=HP, o=2)
            for b in range(B):
                for o in range(2):
                    mm = pe.matmul(M0[64 * o:64 * o + 64, b * 64:(b + 1) * 64], slots(kvnT, b), wv[:, :, o, :],
                                   start=True, stop=True)
            mm.then_inc(S["v"], 1)

            queries_turned(0)
            for p in range(PAIRS):
                pe.wait_ge(S["kadd"], p + 1)
                for j in range(HP):
                    mm = pe.transpose(RB[:, j // 4, (j % 4) * 128:(j % 4 + 1) * 128],
                                      ktok[:, 2 * j:2 * j + 2, :].rearrange("p h d -> p (h d)"), ident)
                mm.then_inc(S["ktp"], 1)
                ctx_scores(2 * p + 1)
                if p >= 2:
                    y3_transpose(p - 2)
                pe.wait_ge(S["qT"], p + 1)
                if p == 0:
                    pe.wait_ge(S["idm"], 2)
                for o in range(2):
                    r = slice(64 * o, 64 * o + SLOT)
                    for j in range(HP):
                        if o == 0 and j % (HP // 2) == 0:
                            pe.wait_ge(S["kT"], 2 * p + 1 + j // (HP // 2))
                        for i in range(2):
                            mm = pe.matmul(RA[i * SLOT:(i + 1) * SLOT, o, j * T:(j + 1) * T],
                                           qT[r, j, i * SLOT:(i + 1) * SLOT], kT[r, j, i * SLOT:i * SLOT + T],
                                           start=(j == 0), stop=False)
                    mm = pe.matmul(RA[:, o, 0:HP * T], identr[:, :], maskr[:, :].unsqueeze(1).broadcast_to([128, HP, T]),
                                   start=False, stop=True)
                    mm.then_inc(S["sc"], 1)
                    if o == 0:
                        ctx_sums(2 * p, 0)
                if p >= 1:
                    y2_transpose(p - 1)
                ctx_sums(2 * p, 1)
                if p >= 1:
                    query_features(p - 1)
                if p < PAIRS - 1:
                    ctx_scores(2 * p + 2)
                    queries(p + 1)
                if p >= 1:
                    cross_out(p - 1)
                pe.wait_ge(S["prb"], 2 * (p + 1))
                for j in range(HP):
                    mm = pe.transpose(RB[:, j // 4, (j % 4) * 128:(j % 4 + 1) * 128],
                                      pr[:, j, :, :].rearrange("p o t -> p (o t)"), ident)
                mm.then_inc(S["ptp"], 1)
                ctx_sums(2 * p + 1, 0)
                if p == 0:
                    pe.wait_ge(S["vv"], 1)
                if p >= 1:
                    pe.wait_ge(S["x1"], p)
                for j in range(HP):
                    if j % (HP // 2) == 0:
                        pe.wait_ge(S["pT"], 2 * p + 1 + j // (HP // 2))
                    for i in range(2):
                        mm = pe.matmul(M0[i * SLOT:(i + 1) * SLOT, j * 2 * VW:(j + 1) * 2 * VW],
                                       pT[:, j, i * SLOT:(i + 1) * SLOT], vv[:, 2 * p + i, j, :], start=True, stop=True)
                mm.then_inc(S["pv"], 1)
                if p < PAIRS - 1:
                    rope_keys(p + 1)
                    content_keys(p + 1)
                else:
                    y3_transpose(p - 1)
                heads_turned(p)
                if p < PAIRS - 1:
                    queries_turned(p + 1)
                ctx_sums(2 * p + 1, 1)
                attn_out(p)

            def product_high(bank, wh, wl, xh, first):
                pe.matmul(bank, wh, xh, start=first, stop=False)
                pe.matmul(bank, wl, xh, start=False, stop=False)

            def product_low(bank, wh, xl, last):
                return pe.matmul(bank, wh, xl, start=False, stop=last)

            def tokens(a, b0, b1):
                return a.rearrange("p q (i t) -> p (q i) t", i=2)[:, b0:b1, 0:T]

            def up_high(c, b0, b1):
                if c % PIECE == 0:
                    pe.wait_ge(S["wl"], c // PIECE + 1)
                product_high(ubank[c % 4][:, b0 * T:b1 * T], wuh[:, c, :], wul[:, c, :], tokens(y3h[:, :, :], b0, b1), True)

            def up_low(c, b0, b1):
                return product_low(ubank[c % 4][:, b0 * T:b1 * T], wuh[:, c, :], tokens(y3l[:, :, :], b0, b1), True)

            def up(c):
                if c >= 4:
                    pe.wait_ge(S["h"], c - 3)
                up_high(c, 0, B)
                up_low(c, 0, B).then_inc(S["up"], 1)

            def router(p):
                return pe.matmul(M0[:, p * E:(p + 1) * E], y3T[:, p, :], col("router"), start=True, stop=True)

            def keep_warm(n):
                for _ in range(n):
                    pe.matmul(K0[:, 0:128], ident, ident, start=True, stop=True)

            def down(c):
                e, j = divmod(c, CHUNKS)
                if j == 0 and e >= 2:
                    pe.wait_ge(S["acc0"], 1) if e == 2 else pe.wait_ge(S["ot"], e - 2)
                if c % PIECE == 0:
                    pe.wait_ge(S["wl"], NPC + c // PIECE + 1)
                pe.wait_ge(S["hh"], c + 1)
                bank = obank[e % 2][:, 0:NT]
                product_high(bank, wdh[:, c, :], wdl[:, c, :], hh[:, c % 4, :], j == 0)
                wait_low(pe, c)
                product_low(bank, wdh[:, c, :], hl[:, c % 4, :], j == CHUNKS - 1).then_inc(S["dn"], 1)

            p, done = PAIRS - 1, B - 2
            for c in range(4):
                up_high(c, 0, done)
            pe.wait_ge(S["y3l"], p)
            for c in range(4):
                up_low(c, 0, done)
            y2_transpose(p)
            for q in range(p):
                router(q)
            query_features(p)
            pe.wait_ge(S["kvs"], B)
            keep_warm(WARM_RFQ)
            cross_out(p)
            keep_warm(WARM_Y3)
            y3_transpose(p)
            keep_warm(WARM_Y3T)
            pe.wait_ge(S["y3T"], 2 * PAIRS)
            router(p).then_inc(S["lg"], 1)
            for c in range(4):
                up_high(c, done, B)
                if c == 0:
                    pe.wait_ge(S["y3l"], PAIRS)
                up_low(c, done, B).then_inc(S["up"], 1)
            for c in range(NCH):
                down(c)
                if c + 4 < NCH:
                    up(c + 4)
                if c == 3:
                    pe.wait_ge(S["cmb"], 1)
                    for p in range(PAIRS):
                        mm = pe.transpose(X0[0:E, p * 128:(p + 1) * 128], sel[:, 4, p, :], ident)
                    mm.then_inc(S["cmtp"], 1)
            for p in range(PAIRS):
                pe.wait_ge(S["accd"], p // 2 + 1)
                mm = pe.transpose(fbank[p // 2][:, p % 2, :], acc[:, 2 * p:2 * p + 2, :].rearrange("p b t -> p (b t)"), ident)
                mm.then_inc(S["ftp"], 1)

        @block.scalar
        def _(act):
            def copy(dst, src, after, n, done, scale=1.0):
                act.wait_ge(S[after], n)
                act.activation(dst, src, ACT.Copy, scale=scale).then_inc(S[done], 1)

            def flat(a):
                return a.rearrange("p a b -> p (a b)")

            def ctx_exp(b):
                act.wait_ge(S["cs"], b + 1)
                if b >= 1:
                    act.wait_ge(S["rft"], b)
                act.activation(rf[:, :], C0[:, 0:GL], ACT.Exp,
                               scale=float(D) ** -0.5).then_inc(S["rf"], 1)

            def ctx_low(b):
                if b >= 1:
                    act.wait_ge(S["kvs"], b)
                copy(kvl[:, :], K0[M:2 * M, 0:2 * CW], "ck", b + 1, "kvl")

            def ctx_high(b):
                act.wait_ge(s_cn[b % RING], 16 * (b // RING + 1))
                if b >= 2:
                    act.wait_ge(S["ck"], b - 1)
                act.activation(ctxsv[:, b % 2, :, 0, :], tiles(b), ACT.Copy).then_inc(S["ch"], 1)

            def weights_high(k):
                act.wait_ge(s_w[k % 2], 16 * (k // 2 + 1))
                j = k % NPC
                act.activation((wuh if k < NPC else wdh)[:, j * PIECE:(j + 1) * PIECE, :], wraw[:, k % 2, :, :],
                               ACT.Copy).then_inc(S["wh"], 1)

            def y3_copies(p):
                copy(y3T[:, p, :], X0[:, 0:128], "y3tp", p + 1, "y3T")
                copy(y3h[:, p, :], X0[:, 0:128], "y3tp", p + 1, "y3T")

            def query_exp(p):
                act.wait_ge(S["rfqp"], p + 1)
                if p >= 1:
                    act.wait_ge(S["xo"], p)
                act.activation(rfq[:, :], X0[0:M, 128:256], ACT.Exp, scale=float(D) ** -0.5).then_inc(S["rfq"], 1)

            copy(flat(yT[:, :, :]), M0[:, :], "yT", 1, "qc")
            ctx_exp(0)
            copy(flat(qcT[:, :, :]), RA[0:QR, 0, :], "kvtok", 2, "kvnT")
            act.wait_ge(s_inB, 48)
            copy(flat(kvnT[:, :, :]), M0[0:KVR, :], "kvtp", 1, "kvnT", scale=p32[:, 256:257])
            def turned_queries(p):
                if p >= 1:
                    act.wait_ge(S["sc"], 2 * p)
                copy(flat(qT[:, :, :]), flat(RA[:, :, :]), "qtp", p + 1, "qT")

            ctx_high(0)
            def halves(dst, after, n, done):
                for g in range(2):
                    copy(flat(dst[:, g * HP // 2:(g + 1) * HP // 2, :]), RB[:, g, :], after, n, done)

            turned_queries(0)
            for p in range(PAIRS):
                if p >= 1:
                    act.wait_ge(S["sc"], 2 * p)
                halves(kT, "ktp", p + 1, "kT")
                ctx_high(2 * p + 1)
                if p < PAIRS - 1:
                    weights_high(PPP * p)
                if p >= 2:
                    y3_copies(p - 2)
                if p >= 1:
                    copy(y2T[:, :], X0[:, 0:128], "y2tp", p, "y2T")
                ctx_exp(2 * p + 1)
                if p >= 1:
                    query_exp(p - 1)
                if p < PAIRS - 1:
                    weights_high(PPP * p + 1)
                act.wait_ge(S["pads"], 2)
                if p >= 1:
                    act.wait_ge(S["ptp"], p)
                for o in range(2):
                    act.wait_ge(S["sub"], 2 * p + o + 1)
                    act.activation(pr[:, :, o, 0:T], sm[:, o, :, :], ACT.Exp, scale=float(QK) ** -0.5).then_inc(S["prb"], 1)
                ctx_low(2 * p)
                if p >= 1:
                    act.wait_ge(S["pv"], p)
                halves(pT, "ptp", p + 1, "pT")
                if p < PAIRS - 1:
                    ctx_exp(2 * p + 2)
                    ctx_high(2 * p + 2)
                else:
                    y3_copies(p - 1)
                copy(atT[:, :], M0[:, 144:272], "atp", p + 1, "atT")
                if p < PAIRS - 1:
                    turned_queries(p + 1)
                ctx_low(2 * p + 1)
                if p < PAIRS - 1:
                    weights_high(PPP * p + 2)
            p = PAIRS - 1
            copy(y2T[:, :], X0[:, 0:128], "y2tp", p + 1, "y2T")
            query_exp(p)
            y3_copies(p)

            def relu(c):
                act.wait_ge(S["up"], c + 1)
                if c >= 2:
                    act.wait_ge(S["h"], c - 1)
                act.activation(rl[c % 2], ubank[c % 4][:, 0:NT], ACT.Relu).then_inc(S["rl"], 1)

            def hidden_high(c):
                act.wait_ge(S["h"], c + 1)
                if c >= 4:
                    act.wait_ge(S["dn"], c - 3)
                act.activation(hh[:, c % 4, :], hf[:, c % 4, :], ACT.Copy).then_inc(S["hh"], 1)

            relu(0)
            act.wait_ge(S["lg"], 1)
            act.activation(gate[:, 0, :, :], M0[:, 0:PAIRS * E].rearrange("p (q e) -> p q e", q=PAIRS), ACT.Exp,
                           scale=-1.0).then_inc(S["en"], 1)
            for c in range(1, NCH):
                relu(c)
                hidden_high(c - 1)
                if c in LATE_AT:
                    weights_high(2 * NPC - LATE + LATE_AT.index(c))
                if c == 6:
                    copy(flat(cT[:, :, :]), X0[0:E, :], "cmtp", 1, "cT")
            hidden_high(NCH - 1)

        @block.gpsimd
        def _(pool):
            pool.memset(mhalf[:, :], -0.5)
            pool.memset(vv[:, :, :, :], 0.0).then_inc(S["pads"], 1)
            pool.memset(qtok[:, :, QK:SLOT], 0.0)
            pool.memset(ktok[:, :, QK:SLOT], 0.0)
            pool.memset(pr[:, :, :, T:SLOT], 0.0).then_inc(S["pads"], 1)

            def power(dst, src, after, n, done):
                pool.wait_ge(S[after], n)
                pool.tensor_tensor(dst, src, mhalf[:, 0:src.shape[1]], ALU.pow).then_inc(S[done], 1)

            pool.wait_ge(S["pads"], 2)
            power(rstd[:, 0, :], vpe[:, 0, :], "ln_eps", 1, "ln_pow")
            power(kvrs[:, :], kvms[:, :], "kvms", 1, "kvpow")

            def low(dst, src, high, done):
                pool.tensor_tensor(dst, src, high.bitcast(F32), ALU.subtract).then_inc(S[done], 1)

            def ctx_lows(b):
                pool.wait_ge(S["ch"], b + 1)
                low(ctxsv[:, b % 2, :, 1, :], tiles(b), ctxsv[:, b % 2, :, 0, :], "cl")

            def weights_low(k):
                pool.wait_ge(S["wh"], k + 1)
                h, l = (wuh, wul) if k < NPC else (wdh, wdl)
                j = k % NPC
                low(l[:, j * PIECE:(j + 1) * PIECE, :], wraw[:, k % 2, :, :], h[:, j * PIECE:(j + 1) * PIECE, :], "wl")

            def ln_power(k, p):
                power(rstd[:, k, p:p + 1], vpe[:, k, p:p + 1], "ln_eps", 2 * p + k + 1, "ln_pow")

            ctx_lows(0)
            for p in range(PAIRS):
                if p >= 1:
                    ln_power(1, p - 1)
                ctx_lows(2 * p + 1)
                if p < PAIRS - 1:
                    weights_low(PPP * p)
                    weights_low(PPP * p + 1)
                if p >= 1:
                    ln_power(2, p - 1)
                if p < PAIRS - 1:
                    ctx_lows(2 * p + 2)
                    weights_low(PPP * p + 2)
            ln_power(1, PAIRS - 1)
            ln_power(2, PAIRS - 1)
            def add_expert(e):
                pool.wait_ge(S["ot"], e)
                if e == 1:
                    pool.wait_ge(S["acc0"], 1)
                else:
                    pool.wait_ge(S["accp"], e - 1)
                pool.tensor_tensor(accv, accv, ot[:, e % 2, :].rearrange("p (b t) -> p b t", b=B),
                                   ALU.add).then_inc(S["accp"], 1)

            for c in range(NCH):
                if on_pool(c):
                    pool.wait_ge(S["hh"], c + 1)
                    if c >= 4:
                        pool.wait_ge(S["dn"], c - 3)
                    low(hl[:, c % 4, :], hf[:, c % 4, :], hh[:, c % 4, :], "hlp")
                if c % CHUNKS == CHUNKS - 1 and 3 * CHUNKS - 1 <= c < NCH - 1:
                    add_expert(c // CHUNKS - 1)
                if c in LATE_AT:
                    weights_low(2 * NPC - LATE + LATE_AT.index(c))

        @block.vector
        def _(v):
            count = {}

            def step(ins, name):
                ins.then_inc(S[name], 1)
                count[name] = count.get(name, 0) + 1

            def own(name):
                v.wait_ge(S[name], count[name])

            def bcast(a, shape):
                return a.unsqueeze(len(a.shape)).broadcast_to(shape)

            def high(dst, src):
                return v.tensor_copy(dst, src)

            def low(dst, src, h):
                return v.tensor_tensor(dst, src, h.bitcast(F32), ALU.subtract)

            def features_split(b):
                v.wait_ge(S["rf"], b + 1)
                if b >= 1:
                    own("rfs")
                step(v.transpose(rft[:, :, :].rearrange("p j m -> p (j m)"), rf[:, :]), "rft")
                if b >= 1:
                    v.wait_ge(S["ck"], b)
                own("rft")
                step(high(rfs[:, :, 0, :], rft[:, :, :]), "fh")
                own("fh")
                step(low(rfs[:, :, 1, :], rft[:, :, :], rfs[:, :, 0, :]), "rfs")

            def ctx_total(b):
                v.wait_ge(S["kvl"], b + 1)
                step(v.tensor_tensor(kvh[:, :], K0[0:M, 0:2 * CW], kvl[:, :], ALU.add), "kvh")
                own("kvh")
                step(v.tensor_tensor(kvs[:, b, :], kvh[:, 0:D + 1], kvh[:, CW:CW + D + 1], ALU.add), "kvs")

            def y3_low(p):
                v.wait_ge(S["y3T"], 2 * p + 2)
                step(low(y3l[:, p, :], y3T[:, p, :], y3h[:, p, :]), "y3l")

            def ln_stats(x, k, p):
                step(v.bn_stats(stats[:, k, p, :], x), "ln_stat")
                own("ln_stat")
                step(v.bn_aggr(mv[:, k, p, :], stats[:, k, p, :]), "ln_stat")

            def ln_eps(k, p0, p1):
                own("ln_stat")
                step(v.tensor_scalar(vpe[:, k, p0:p1], mv[:, k, p0:p1, 1], LN_EPS, None, ALU.add), "ln_eps")

            def ln_apply(dst, x, k, p):
                return v.tensor_scalar(dst, x, mv[:, k, p, 0:1], rstd[:, k, p:p + 1], ALU.subtract, ALU.mult)

            v.wait_ge(s_x, 16)
            for p in range(PAIRS):
                step(v.bn_stats(stats[:, 0, p, :], xin[:, p, :]), "ln_stat")
            own("ln_stat")
            for p in range(PAIRS):
                step(v.bn_aggr(mv[:, 0, p, :], stats[:, 0, p, :]), "ln_stat")
            ln_eps(0, 0, PAIRS)
            v.wait_ge(S["ln_pow"], 1)
            for p in range(PAIRS):
                step(ln_apply(y1[:, p, :], xin[:, p, :], 0, p), "y1")
            step(high(identr[:, :], ident), "idm")
            v.wait_ge(S["kvtok"], 1)
            step(v.tensor_copy(kvt[:, :, :].rearrange("p a b -> p (a b)"), X0[:, 0:PAIRS * KVR]), "kvcp")
            own("kvcp")
            step(v.tensor_tensor(kvsq[:, :, :], kvt[:, :, :], kvt[:, :, :], ALU.mult), "kvsq")
            own("kvsq")
            step(v.tensor_reduce(kvss[:, :], kvsq[:, :, :], AX_X, ALU.add), "kvss")
            own("kvss")
            step(v.tensor_scalar(kvms[:, :], kvss[:, :], 1.0 / KVR, RMS_EPS, ALU.mult, ALU.add), "kvms")
            v.wait_ge(S["kvpow"], 1)
            step(v.tensor_tensor(kvn[:, :, :], kvt[:, :, :], bcast(kvrs[:, :], [128, PAIRS, KVR]), ALU.mult), "kvn")
            v.wait_ge(S["pads"], 2)
            v.memset(vv[0:64, :, :, HD:HD + 1], 1.0)
            v.memset(vv[64:128, :, :, VW + HD:VW + HD + 1], 1.0)

            def heads(region):
                return region[:, :, 0:8 * QK].rearrange("p g (h d) -> p g h d", h=8)

            def rotate(region, tok, t1, t2, source, done, n):
                src = heads(region)
                th = tok[:, :, :].rearrange("p (g h) d -> p g h d", g=2)
                c4 = [128, 2, 8, RD]
                half = [128, 2, 8, RD // 2]

                def table(name, a, b, shape):
                    return col(name)[:, a:b].unsqueeze(1).unsqueeze(1).broadcast_to(shape)

                v.wait_ge(S[source], n)
                r1 = t1[:, :, :].rearrange("p (g h) d -> p g h d", g=2)
                r2 = t2[:, :, :].rearrange("p (g h) d -> p g h d", g=2)
                v.tensor_tensor(r1, src[:, :, :, HD:QK], table("cos", 0, RD, c4), ALU.mult)
                step(v.tensor_tensor(r2[:, :, :, 0:16], src[:, :, :, HD + 16:QK], table("sin", 0, 16, half), ALU.mult), done)
                step(v.tensor_tensor(r2[:, :, :, 16:32], src[:, :, :, HD:HD + 16], table("sin", 16, 32, half), ALU.mult), done)
                step(v.tensor_copy(th[:, :, :, 0:HD], src[:, :, :, 0:HD]), done)

            def attn_norm(p):
                v.wait_ge(S["pv"], p + 1)
                a = M0[:, 0:HP * 2 * VW].rearrange("p (h d) -> p h d", h=H)
                step(v.reciprocal(rs[:, :], a[:, :, HD]), "rsum")
                own("rsum")
                if p >= 1:
                    v.wait_ge(S["atp"], p)
                step(v.tensor_tensor(at[:, :, :], a[:, :, 0:HD], bcast(rs[:, :], [128, H, HD]), ALU.mult), "atn")

            def residual1(p):
                v.wait_ge(S["wo"], p + 1)
                step(v.tensor_tensor(x1[:, p, :], M0[:, 272:400], xin[:, p, :], ALU.add), "x1")
                own("x1")
                ln_stats(x1[:, p, :], 1, p)
                ln_eps(1, p, p + 1)

            def norm2(p):
                v.wait_ge(S["ln_pow"], 2 * p + 2)
                if p >= 1:
                    v.wait_ge(S["y2tp"], p)
                step(ln_apply(y2[:, :], x1[:, p, :], 1, p), "y2")

            def residual2(p):
                v.wait_ge(S["xo"], p + 1)
                step(v.tensor_scalar(den[:, 0:1], X0[:, 256 + D:257 + D], XN_EPS * float(M) ** 0.5, None, ALU.add), "den")
                own("den")
                step(v.reciprocal(den[:, 1:2], den[:, 0:1]), "drec")
                own("drec")
                step(v.scalar_tensor_tensor(out=x2[:, p, :], in0=X0[:, 256:256 + D], scalar=den[:, 1:2], in1=x1[:, p, :],
                                            op0=ALU.mult, op1=ALU.add), "x2")
                own("x2")
                ln_stats(x2[:, p, :], 2, p)
                ln_eps(2, p, p + 1)

            def norm3(p):
                v.wait_ge(S["ln_pow"], 2 * p + 3)
                if p >= 1:
                    v.wait_ge(S["y3tp"], p)
                step(ln_apply(y3[:, :], x2[:, p, :], 2, p), "y3")

            def turn_queries(p):
                if p >= 1:
                    v.wait_ge(S["qtp"], p)
                    own("kadd")
                rotate(RA, qtok, rt[0], rt[1], "pq", "rq", p + 1)
                own("rq")
                step(v.tensor_tensor(qtok[:, :, HD:QK], rt[0][:, :, :], rt[1][:, :, :], ALU.add), "qadd")

            def turn_keys(p):
                own("qadd")
                if p >= 1:
                    v.wait_ge(S["ktp"], p)
                rotate(RB, ktok, rt[0], rt[1], "pk", "rk", p + 1)
                own("rk")
                step(v.tensor_tensor(ktok[:, :, HD:QK], rt[0][:, :, :], rt[1][:, :, :], ALU.add), "kadd")

            v.wait_ge(s_inB, 48)
            step(high(maskr[:, :], col("mask")), "idm")
            turn_queries(0)
            for p in range(PAIRS):
                turn_keys(p)
                if p >= 1:
                    residual1(p - 1)
                    ctx_total(2 * p - 1)
                features_split(2 * p)
                if p == 0:
                    v.wait_ge(S["v"], 1)
                    for o in range(2):
                        src = M0[64 * o:64 * o + 64, :].rearrange("p (b j d) -> p b j d", b=B, j=HP)
                        ins = v.tensor_copy(vv[64 * o:64 * o + 64, :, :, o * VW:o * VW + HD], src)
                    step(ins, "vv")
                if p >= 1:
                    norm2(p - 1)
                if p >= 1:
                    v.wait_ge(S["prb"], 2 * p)
                wide = [128, HP, T]
                for o in range(2):
                    v.wait_ge(S["sc"], 2 * p + o + 1)
                    scores = RA[:, o, 0:HP * T].rearrange("p (j t) -> p j t", j=HP)
                    step(v.tensor_reduce(mx[:, o, :], scores, AX_X, ALU.max), "smx")
                    own("smx")
                    step(v.tensor_tensor(sm[:, o, :, :], scores, bcast(mx[:, o, :], wide), ALU.subtract), "sub")
                features_split(2 * p + 1)
                ctx_total(2 * p)
                if p < PAIRS - 1:
                    turn_queries(p + 1)
                if p >= 1:
                    residual2(p - 1)
                if p >= 2:
                    y3_low(p - 2)
                attn_norm(p)
                if p >= 1:
                    norm3(p - 1)
            p = PAIRS - 1
            residual1(p)
            y3_low(p - 1)
            norm2(p)
            ctx_total(2 * p + 1)
            residual2(p)
            norm3(p)
            y3_low(p)

            def hidden(c):
                v.wait_ge(S["rl"], c + 1)
                if c >= 4:
                    v.wait_ge(S["hh"], c - 3)
                    wait_low(v, c - 4)
                step(v.scalar_tensor_tensor(out=hf[:, c % 4, :], in0=ubank[c % 4][:, 0:NT], scalar=0.0, in1=rl[c % 2],
                                            op0=ALU.max, op1=ALU.mult), "h")

            def hidden_low(c):
                if on_pool(c):
                    return
                v.wait_ge(S["hh"], c + 1)
                if c >= 4:
                    v.wait_ge(S["dn"], c - 3)
                step(low(hl[:, c % 4, :], hf[:, c % 4, :], hh[:, c % 4, :]), "hlv")

            def tok(a):
                return a.rearrange("p (b t) -> p b t", b=B)

            def expert_out(e):
                v.wait_ge(S["dn"], CHUNKS * (e + 1))
                if e == 0:
                    step(v.tensor_copy(accv, tok(obank[0][:, 0:NT])), "acc0")
                    return
                v.wait_ge(s_cb[e > 2], 16 * (2 if e <= 2 else E - 2))
                if e >= 3:
                    v.wait_ge(S["accp"], e - 2)
                if e < E:
                    step(v.tensor_tensor(ot[:, e % 2, :], obank[e % 2][:, 0:NT], cb[:, e - 1, :], ALU.mult), "ot")
                    return
                for k in range(2):
                    t = slice(k * NT // 2, (k + 1) * NT // 2)
                    half = accv[:, k * B // 2:(k + 1) * B // 2, :]
                    step(v.tensor_tensor(ot[:, e % 2, t], obank[e % 2][:, t], cb[:, e - 1, t], ALU.mult), "ot")
                    own("ot")
                    step(v.tensor_tensor(half, half, ot[:, e % 2, t].rearrange("p (b t) -> p b t", b=B // 2), ALU.add), "accd")

            shape = [128, PAIRS, E]

            def choose_probs():
                v.memset(acc[:, :, T:SLOT], 0.0)
                v.wait_ge(S["en"], 1)
                step(v.tensor_scalar(gate[:, 1, :, :], gate[:, 0, :, :], 1.0, None, ALU.add), "one")
                own("one")
                step(v.reciprocal(gate[:, 2, :, :], gate[:, 1, :, :]), "prbs")

            def choose_top():
                own("prbs")
                for p in range(PAIRS):
                    step(v.max(top[:, p, :], gate[:, 2, p, :]), "topv")
                own("topv")
                for p in range(PAIRS):
                    step(v.max_index(topi[:, p, :], top[:, p, :], gate[:, 2, p, :]), "topx")

            def choose_share():
                own("topx")
                step(v.tensor_copy(topf[:, :, :], topi[:, :, 0:2]), "topf")
                step(v.tensor_tensor(tden[:, 0, :], top[:, :, 0], top[:, :, 1], ALU.add), "dsum")
                own("dsum")
                step(v.tensor_scalar(tden[:, 1, :], tden[:, 0, :], TOPK_EPS, None, ALU.add), "dsum")
                own("dsum")
                step(v.reciprocal(tden[:, 2, :], tden[:, 1, :]), "drc")
                own("topf")
                iota = col("iota").unsqueeze(1).broadcast_to(shape)
                for k in range(2):
                    step(v.tensor_tensor(sel[:, k, :, :], iota, bcast(topf[:, :, k], shape), ALU.is_equal), "selc")

            def choose_weights():
                own("selc")
                for k in range(2):
                    step(v.tensor_tensor(sel[:, 2 + k, :, :], sel[:, k, :, :], bcast(top[:, :, k], shape), ALU.mult), "selc")
                own("selc")
                step(v.tensor_tensor(sel[:, 0, :, :], sel[:, 2, :, :], sel[:, 3, :, :], ALU.add), "selc")
                own("selc")
                own("drc")
                step(v.tensor_tensor(sel[:, 4, :, :], sel[:, 0, :, :], bcast(tden[:, 2, :], shape), ALU.mult), "cmb")

            for c in range(NCH):
                hidden(c)
                if c >= 1:
                    hidden_low(c - 1)
                if 1 <= c <= 4:
                    (choose_probs, choose_top, choose_share, choose_weights)[c - 1]()
                if c % CHUNKS == CHUNKS - 1 and c > CHUNKS:
                    expert_out(c // CHUNKS - 1)
            hidden_low(NCH - 1)
            own("ot")
            v.wait_ge(S["accp"], E - 2)
            step(v.tensor_tensor(accv, accv, tok(ot[:, (E - 1) % 2, :]), ALU.add), "acc7")
            own("acc7")
            expert_out(E)
            for k in range(2):
                v.wait_ge(S["ftp"], 2 * k + 2)
                step(v.tensor_tensor(fin[:, 2 * k:2 * k + 2, :], fbank[k],
                                     x2[:, 2 * k:2 * k + 2, :], ALU.add), "fin")


def _constants():
    mask = np.zeros((2, SLOT, T), np.float32)
    mask[:, :T] = np.where(np.tril(np.ones((T, T), bool)), 0.0, NEG)
    inv_freq = 1.0 / 10000.0 ** (np.arange(0, RD, 2, dtype=np.float32) / RD)
    freqs = np.outer(np.arange(T, dtype=np.float32), inv_freq)
    cos, sin = np.zeros((2, SLOT, RD), np.float32), np.zeros((2, SLOT, RD), np.float32)
    cos[:, :T] = np.cos(np.concatenate([freqs, freqs], -1))
    sin[:, :T] = np.sin(np.concatenate([-freqs, freqs], -1))
    return {
        "ident": np.eye(128, dtype=np.float32), "mask": mask.reshape(128, T), "cos": cos.reshape(128, RD),
        "sin": sin.reshape(128, RD), "iota": np.tile(np.arange(E, dtype=np.float32), (128, 1)),
    }


def kernel(x, ctx_1024, L0_attn_W_kv, L0_attn_g_kv, L0_attn_W_kdec, L0_attn_W_vdec, L0_attn_W_q, L0_attn_W_qdec,
           L0_attn_W_krope, L0_attn_W_qrope, L0_attn_W_o, L0_xattn_projection, L0_ffn_W_router, L0_ffn_W_up,
           L0_ffn_W_down, L0_ffn_W_sh_up, L0_ffn_W_sh_down):
    import concourse.bacc as _bacc
    from concourse.bass_utils import run_bass_kernel_spmd as _run

    a = {k: np.asarray(v) for k, v in locals().items() if k[0] != "_"}
    xp = np.zeros((PAIRS, 2, SLOT, D), np.float32)
    xp[:, :, :T] = a["x"].reshape(PAIRS, 2, T, D)
    parts = _constants() | {
        "xpad": xp.reshape(PAIRS, 128, D).transpose(1, 0, 2).reshape(128, PAIRS * D),
        "wkv": a["L0_attn_W_kv"], "wq": a["L0_attn_W_q"], "krope": a["L0_attn_W_krope"], "wo": a["L0_attn_W_o"],
        "proj": a["L0_xattn_projection"].T, "router": a["L0_ffn_W_router"],
    }
    pack128 = np.concatenate([parts[k] for k in W128], 1)
    wqcat = np.concatenate([a["L0_attn_W_qdec"].reshape(QR, H, HD), a["L0_attn_W_qrope"].reshape(QR, H, RD)], 2)
    pack32 = np.concatenate([a["L0_attn_W_kdec"], a["L0_attn_W_vdec"], a["L0_attn_g_kv"].reshape(KVR, 1)], 1)
    c = np.zeros((B, GR * GL, CW), np.float32)
    c[:, :L, :D] = a["ctx_1024"]
    c[:, :L, D:] = 1.0
    ctx_nat = c.reshape(B, GR, CT, 32, CW).transpose(0, 1, 3, 2, 4).reshape(B, 128, CT * CW)
    ctx_tr = c[:, :, :D].transpose(0, 2, 1).reshape(B, D, GR, GL)
    up = np.concatenate([a["L0_ffn_W_sh_up"][None], a["L0_ffn_W_up"]], 0).reshape(E + 1, D, CHUNKS, 128)
    down = np.concatenate([a["L0_ffn_W_sh_down"][None], a["L0_ffn_W_down"]], 0).reshape(NCH, 128, D)
    arrays = {
        "pack128": pack128, "wqcat": wqcat.reshape(QR, H * QK), "pack32": pack32, "ctx_nat": ctx_nat, "ctx_tr": ctx_tr,
        "w_up": up.transpose(1, 0, 2, 3).reshape(D, NCH, 128), "w_down": down.transpose(1, 0, 2),
    }
    arrays = {k: np.ascontiguousarray(v) for k, v in arrays.items()}
    nc = _bacc.Bacc("TRN2", target_bir_lowering=False, num_devices=1)
    args = [nc.dram_tensor(k, v.shape, mybir.dt.from_np(v.dtype), kind="ExternalInput").ap() for k, v in arrays.items()]
    out = nc.dram_tensor("out", (128, PAIRS, D), F32, kind="ExternalOutput").ap()
    share = nc.dram_tensor("share", (E, B, T), F32, kind="Internal").ap()
    decoder_layer(nc, *args, share, out)
    got = _run(nc, [arrays], core_ids=[0]).results[0]["out"]
    return got.reshape(2, SLOT, PAIRS, D).transpose(2, 0, 1, 3)[:, :, :T].reshape(B, T, D)
```

```python
from contextlib import ExitStack

import concourse.bass as bass
from concourse import mybir
import numpy as np

F32 = mybir.dt.float32
F32R = mybir.dt.float32r
U32 = mybir.dt.uint32
ALU = mybir.AluOpType
ACT = mybir.ActivationFunctionType
AX_X = mybir.AxisListType.X

B, T, D = 8, 56, 128
H, HD, RD = 16, 8, 32
KVR, QR = 32, 64
L, M = 1500, 32
E, HID = 8, 512
LN_EPS, RMS_EPS, XN_EPS, TOPK_EPS = 1e-5, 1e-6, 1e-6, 1e-6

SLOT = 64
PAIRS = B // 2
QK = HD + RD
HP = H // 2
VW = HD + 1
NT = B * T
GR = 4
CT = -(-L // 128)
GL = CT * 32
CW = D + 2
RING = 2
CHUNKS = HID // 128
NCH = (E + 1) * CHUNKS
PIECE = 6
NPC = NCH // PIECE
PPP = 2 * NPC // PAIRS
AHEAD = 3
DONE = (B - 2) * T
LATE = 3
LATE_AT = (3, 11, 19)
WARM = 3
WARM_KV, WARM_KT = 4, 2
WARM_RFQ, WARM_Y3 = 2, 2
NEG = -3.0e38

W128 = dict(xpad=PAIRS * 128, ident=128, wkv=KVR, wq=QR, proj=M, krope=H * RD, wo=D, router=E, mask=T, cos=RD, sin=RD, iota=E)
COL = {}
for _k, _n in W128.items():
    COL[_k] = (sum(v for v in list(W128.values())[:len(COL)]), _n)
N_X = W128["xpad"]
N_A = N_X + sum(W128[k] for k in ("ident", "wkv", "wq", "proj"))
N_W = sum(W128.values())


def decoder_layer(nc, pack128, wqcat, pack32, ctx_nat, ctx_tr, w_up, w_down, share, out):
    with ExitStack() as stack:
        def sb(name, shape, dt=F32):
            return stack.enter_context(nc.sbuf_tensor(name, shape, dt))

        def sem(name):
            return stack.enter_context(nc.semaphore(name))

        pk = sb("pk", [128, N_W])
        identr = sb("identr", [128, 128], F32R)
        maskr = sb("maskr", [128, T], F32R)
        wqc = sb("wqc", [QR, H * QK])
        p32 = sb("p32", [KVR, 2 * H * HD + 1])
        ctxs = sb("ctxs", [128, 2 * CT * 2 * CW], F32R)
        craw = sb("craw", [128, RING * (GR * GL + CT * CW)])
        wraw = sb("wraw", [128, 2, PIECE, 128])
        wuh, wul = sb("wuh", [128, NCH, 128], F32R), sb("wul", [128, NCH, 128], F32R)
        wdh, wdl = sb("wdh", [128, NCH, 128], F32R), sb("wdl", [128, NCH, 128], F32R)
        stats = sb("stats", [128, 3, PAIRS, 6])
        mv = sb("mv", [128, 3, PAIRS, 2])
        vpe = sb("vpe", [128, 3, PAIRS])
        rstd = sb("rstd", [128, 3, PAIRS])
        mhalf = sb("mhalf", [128, PAIRS])
        y1 = sb("y1", [128, PAIRS, 128])
        yT = sb("yT", [128, PAIRS, 128])
        qcT = sb("qcT", [QR, PAIRS, 128])
        kvss = sb("kvss", [128, PAIRS])
        kvms = sb("kvms", [128, PAIRS])
        kvrs = sb("kvrs", [128, PAIRS])
        kvnT = sb("kvnT", [KVR, PAIRS, 128])
        vv = sb("vv", [128, B, HP, 2 * VW])
        rt = [sb(f"rt{i}", [128, H, RD]) for i in range(2)]
        qtok = sb("qtok", [128, H, SLOT])
        ktok = sb("ktok", [128, H, SLOT])
        qT = sb("qT", [128, HP, 128])
        kT = sb("kT", [128, HP, 128])
        sm = sb("sm", [128, 2, HP, T])
        mx = sb("mx", [128, 2, HP])
        pr = sb("pr", [128, HP, 2, SLOT])
        pT = sb("pT", [128, HP, 128])
        rs = sb("rs", [128, H])
        at = sb("at", [128, H, HD])
        atT = sb("atT", [128, 128])
        x1 = sb("x1", [128, PAIRS, 128])
        y2 = sb("y2", [128, 128])
        y2T = sb("y2T", [128, 128])
        rfq = sb("rfq", [M, 128])
        rf = sb("rf", [128, GL])
        rft = sb("rft", [128, CT, M])
        rfs = sb("rfs", [128, CT, 2, M], F32R)
        kvlh = sb("kvlh", [2 * M, 2 * CW])
        kvs = sb("kvs", [M, B, D + 1])
        den = sb("den", [128, 2])
        x2 = sb("x2", [128, PAIRS, 128])
        y3 = sb("y3", [128, 128])
        y3T = sb("y3T", [128, PAIRS, 128])
        y3h, y3l = sb("y3h", [128, PAIRS, 128], F32R), sb("y3l", [128, PAIRS, 128], F32R)
        gate = sb("gate", [128, 3, PAIRS, E])
        top = sb("top", [128, PAIRS, 8])
        topi = sb("topi", [128, PAIRS, 8], U32)
        topf = sb("topf", [128, PAIRS, 2])
        tden = sb("tden", [128, 3, PAIRS])
        sel = sb("sel", [128, 5, PAIRS, E])

        RA = stack.enter_context(nc.psum_tensor("RA", [128, 2, 512], F32))
        RB = stack.enter_context(nc.psum_tensor("RB", [128, 2, 512], F32))
        M0 = stack.enter_context(nc.psum_tensor("M0", [128, 512], F32))
        X0 = stack.enter_context(nc.psum_tensor("X0", [128, 512], F32))
        C0 = stack.enter_context(nc.psum_tensor("C0", [128, 512], F32))
        K0 = stack.enter_context(nc.psum_tensor("K0", [128, 512], F32))

        cb = craw[:, 0:E * NT].rearrange("p (e t) -> p e t", e=E)
        hf = craw[:, E * NT:(E + 4) * NT].rearrange("p (k t) -> p k t", k=4)
        hh, hl = (ctxs[:, k * 4 * NT:(k + 1) * 4 * NT].rearrange("p (k t) -> p k t", k=4) for k in range(2))
        rl = [a[:, :, :].rearrange("p h d -> p (h d)")[:, 0:NT] for a in rt]
        ot = qT[:, :, :].rearrange("p j t -> p (j t)")[:, 0:2 * NT].rearrange("p (k t) -> p k t", k=2)
        cT = kT[0:E, 0:4, :]
        acc = kT[:, 4:8, :].rearrange("p q (i t) -> p (q i) t", i=2)
        accv = acc[:, :, 0:T]
        end = pr[:, 0:4, :, :].rearrange("p j o t -> p (j o) t")
        fin = y1
        kvt, kvsq, kvn = (x1[:, k, :].rearrange("p (q d) -> p q d", q=PAIRS) for k in range(3))
        kvl, kvh = kvlh[0:M, :], kvlh[M:2 * M, :]
        ctxn = craw[:, RING * GR * GL:].rearrange("p (r d) -> p r d", r=RING)
        ctxtv = craw[:, 0:RING * GR * GL].rearrange("p (r g t) -> p r g t", r=RING, g=GR)
        ctxsv = ctxs[:, :].rearrange("p (r j k d) -> p r j k d", r=2, j=CT, k=2)
        ubank = [RA[:, 0, :], RA[:, 1, :], RB[:, 0, :], RB[:, 1, :], M0[:, :]]
        UB = len(ubank)
        obank = [C0[:, :], K0[:, :]]
        fbank = [a[:, 0:256].rearrange("p (q d) -> p q d", q=2) for a in (X0, M0)]

        def on_pool(c):
            return c % 8 in (1, 3, 7) and c < NCH - 2

        def nth(c):
            return c + AHEAD

        def piece(n):
            return n if n < AHEAD else n - AHEAD

        def span(n):
            return slice(0, DONE) if n < AHEAD else slice(DONE, NT) if piece(n) < AHEAD else slice(0, NT)

        def low_count(n):
            return sum(on_pool(piece(k)) == on_pool(piece(n)) for k in range(n + 1))

        def wait_low(engine, n):
            engine.wait_ge(S["hlp"] if on_pool(piece(n)) else S["hlv"], low_count(n))

        def tiles(b):
            return ctxn[:, b % RING, :].rearrange("p (j d) -> p j d", j=CT)

        def col(name):
            a, n = COL[name]
            return pk[:, a:a + n]

        ident = col("ident")
        xin = col("xpad").rearrange("p (q d) -> p q d", q=PAIRS)

        s_x, s_inA, s_inB, s_out = sem("s_x"), sem("s_inA"), sem("s_inB"), sem("s_out")
        s_share = sem("s_share")
        s_cb = [sem("s_cb0"), sem("s_cb1")]
        s_cn = [sem(f"s_cn{i}") for i in range(RING)]
        s_ct = [sem(f"s_ct{i}") for i in range(RING)]
        s_w = [sem("s_w0"), sem("s_w1")]
        names = """pads ln_stat ln_mean ln_eps ln_pow y1 yT qc kvtok kvcp kvsq kvss kvms kvpow kvn kvtp kvnT v vv
            pq pk rq rk qadd kadd qtp ktp qT kT sc idm smx sub prb ptp pT pv rsum atn atp atT wo x1 y2 y2tp y2T
            rfqp rfq xo den drec x2 y3 y3tp y3T y3l cs rf rft fh rfs ch cl ck kvl kvh kvs wh wl lg en one prbs topv topx topf dsum drc selc cmb
            cmtp cT up rl h hh hlv hlp dn ot acc0 accp ftp fin""".split()
        S = {n: sem("s_" + n) for n in names}

        block = stack.enter_context(nc.Block())

        @block.sync
        def _(sp):
            sp.dma_start(pk[:, 0:N_X], pack128[:, 0:N_X]).then_inc(s_x, 16)
            sp.dma_start(pk[:, N_X:N_A], pack128[:, N_X:N_A]).then_inc(s_inA, 16)

            def context_t(b):
                if b >= RING:
                    sp.wait_ge(S["cs"], b - RING + 1)
                sp.dma_start(ctxtv[:, b % RING, :, :], ctx_tr[b]).then_inc(s_ct[b % RING], 16)

            def context_n(b):
                if b >= RING:
                    sp.wait_ge(S["cl"], b - RING + 1)
                sp.dma_start(ctxn[:, b % RING, :], ctx_nat[b]).then_inc(s_cn[b % RING], 16)

            def weights(k):
                if k >= 2:
                    sp.wait_ge(S["wl"], k - 1)
                src = w_up if k < NPC else w_down
                j = k % NPC
                sp.dma_start(wraw[:, k % 2, :, :], src[:, j * PIECE:(j + 1) * PIECE, :]).then_inc(s_w[k % 2], 16)

            context_t(0)
            sp.dma_start(pk[:, N_A:N_W], pack128[:, N_A:N_W]).then_inc(s_inB, 16)
            sp.dma_start(wqc[:, :], wqcat).then_inc(s_inB, 16)
            sp.dma_start(p32[:, :], pack32).then_inc(s_inB, 16)
            context_n(0)
            k = 0
            for b in range(1, B):
                context_t(b)
                context_n(b)
                for _ in range((0, 2, 0, 2, 1, 2, 1, 3)[b]):
                    weights(k)
                    k += 1
            assert k == 2 * NPC - 1
            sp.wait_ge(S["cT"], 1)
            sp.dma_start(share, cT[:, :, :].rearrange("p q (i t) -> p (q i) t", i=2)[:, :, 0:T]).then_inc(s_share, 16)
            sp.wait_ge(s_share, 16)
            for e in range(E):
                sp.dma_start(cb[:, e, :], share[e:e + 1, :, :].rearrange("e b t -> e (b t)").broadcast_to([128, NT])).then_inc(s_cb[e > 1], 16)
            weights(k)
            for k in range(2):
                sp.wait_ge(S["fin"], k + 1)
                sp.dma_start(out[:, 2 * k:2 * k + 2, :], fin[:, 2 * k:2 * k + 2, :]).then_inc(s_out, 16)
            sp.wait_ge(s_out, 32)

        @block.tensor
        def _(pe):
            def slots(a, b):
                return a[:, b // 2, (b % 2) * SLOT:(b % 2) * SLOT + SLOT]

            def ctx_scores(b):
                pe.wait_ge(s_ct[b % RING], 16 * (b // RING + 1))
                if b >= 1:
                    pe.wait_ge(S["rf"], b)
                for g in range(GR):
                    mm = pe.matmul(C0[M * g:M * (g + 1), 0:GL], col("proj"), ctxtv[:, b % RING, g, :], start=True, stop=True)
                mm.then_inc(S["cs"], 1)

            def ctx_sums(b, half):
                if half == 0:
                    pe.wait_ge(S["rfs"], b + 1)
                    pe.wait_ge(S["cl"], b + 1)
                    if b >= 1:
                        pe.wait_ge(S["kvs"], b)
                for j in range(half * CT // 2, (half + 1) * CT // 2):
                    mm = pe.matmul(K0[0:2 * M, 0:2 * CW], rfs[:, j, :, :].rearrange("p k m -> p (k m)"),
                                   ctxsv[:, b % 2, j, :, :].rearrange("p k d -> p (k d)"), start=(j == 0), stop=(j == CT - 1))
                if half == 1:
                    mm.then_inc(S["ck"], 1)

            def keep_warm(n):
                for _ in range(n):
                    pe.matmul(K0[:, 0:128], ident, ident, start=True, stop=True)

            def queries(p):
                if p >= 1:
                    pe.wait_ge(S["sub"], 2 * p)
                for g in range(2):
                    mm = pe.matmul(RA[:, g, 0:8 * QK], qcT[:, p, :], wqc[:, g * 8 * QK:(g + 1) * 8 * QK], start=True, stop=True)
                mm.then_inc(S["pq"], 1)

            def key_heads(g):
                return RB[:, g, 0:8 * QK].rearrange("p (h d) -> p h d", h=8)

            def queries_turned(p):
                if p == 0:
                    pe.wait_ge(S["pads"], 2)
                pe.wait_ge(S["qadd"], p + 1)
                pe.wait_ge(S["rq"], 3 * (p + 1))
                for j in range(HP):
                    mm = pe.transpose(RA[:, j // 4, (j % 4) * 128:(j % 4 + 1) * 128],
                                      qtok[:, 2 * j:2 * j + 2, :].rearrange("p h d -> p (h d)"), ident)
                mm.then_inc(S["qtp"], 1)

            def rope_keys(p):
                if p >= 1:
                    pe.wait_ge(S["pT"], 2 * p)
                for g in range(2):
                    pe.matmul(key_heads(g)[:, :, HD:QK], yT[:, p, :], col("krope")[:, g * 256:(g + 1) * 256], start=True, stop=True)

            def content_keys(p):
                for g in range(2):
                    mm = pe.matmul(key_heads(g)[:, :, 0:HD], kvnT[:, p, :], p32[:, g * 64:(g + 1) * 64], start=True, stop=True)
                mm.then_inc(S["pk"], 1)

            def heads_turned(p):
                pe.wait_ge(S["atn"], p + 1)
                pe.transpose(M0[:, 144:272], at[:, :, :].rearrange("p h d -> p (h d)"), ident).then_inc(S["atp"], 1)

            def attn_out(p):
                pe.wait_ge(S["atT"], p + 1)
                pe.matmul(M0[:, 272:400], atT[:, :], col("wo"), start=True, stop=True).then_inc(S["wo"], 1)

            def y2_transpose(p):
                pe.wait_ge(S["y2"], p + 1)
                if p >= 1:
                    pe.wait_ge(S["y3T"], 2 * p)
                pe.transpose(X0[:, 0:128], y2[:, :], ident).then_inc(S["y2tp"], 1)

            def query_features(p):
                pe.wait_ge(S["y2T"], p + 1)
                pe.matmul(X0[0:M, 128:256], col("proj"), y2T[:, :], start=True, stop=True).then_inc(S["rfqp"], 1)

            def cross_out(p):
                pe.wait_ge(S["rfq"], p + 1)
                pe.wait_ge(S["kvs"], 2 * p + 2)
                for i in range(2):
                    mm = pe.matmul(X0[i * SLOT:(i + 1) * SLOT, 256:256 + D + 1], rfq[:, i * SLOT:(i + 1) * SLOT],
                                   kvs[:, 2 * p + i, :], start=True, stop=True)
                mm.then_inc(S["xo"], 1)

            def y3_transpose(p):
                pe.wait_ge(S["y3"], p + 1)
                pe.transpose(X0[:, 0:128], y3[:, :], ident).then_inc(S["y3tp"], 1)

            pe.wait_ge(S["pads"], 1)
            for _ in range(WARM):
                pe.matmul(K0[:, :], vv[:, 0:2, :, :].rearrange("p b j d -> p (b j d)")[:, 0:128],
                          vv[:, :, :, :].rearrange("p b j d -> p (b j d)")[:, 0:512], start=True, stop=True)
            pe.wait_ge(s_inA, 16)
            for p in range(PAIRS):
                pe.wait_ge(S["y1"], p + 1)
                mm = pe.transpose(M0[:, p * 128:(p + 1) * 128], y1[:, p, :], ident)
            mm.then_inc(S["yT"], 1)
            ctx_scores(0)
            pe.wait_ge(S["qc"], 1)
            for p in range(PAIRS):
                mm = pe.matmul(X0[:, p * KVR:(p + 1) * KVR], yT[:, p, :], col("wkv"), start=True, stop=True)
            mm.then_inc(S["kvtok"], 1)
            pe.matmul(RA[0:QR, 0, :], col("wq"), yT[:, :, :].rearrange("p q t -> p (q t)"), start=True, stop=True).then_inc(S["kvtok"], 1)
            pe.wait_ge(s_inB, 48)
            pe.wait_ge(S["kvnT"], 1)
            queries(0)
            rope_keys(0)
            ctx_scores(1)
            pe.wait_ge(S["kvn"], 1)
            for p in range(PAIRS):
                mm = pe.transpose(M0[0:KVR, p * 128:(p + 1) * 128], kvn[:, p, :], ident)
            mm.then_inc(S["kvtp"], 1)
            keep_warm(WARM_KV)
            pe.wait_ge(S["kvnT"], 2)
            content_keys(0)
            queries_turned(0)
            wv = p32[:, H * HD:2 * H * HD].rearrange("p (j o d) -> p j o d", j=HP, o=2)
            for b in range(B):
                for o in range(2):
                    mm = pe.matmul(M0[64 * o:64 * o + 64, b * 64:(b + 1) * 64], slots(kvnT, b), wv[:, :, o, :],
                                   start=True, stop=True)
            mm.then_inc(S["v"], 1)

            for p in range(PAIRS):
                for j in range(HP):
                    if j % (HP // 2) == 0:
                        pe.wait_ge(S["kadd"], 2 * p + 1 + j // (HP // 2))
                    mm = pe.transpose(RB[:, j // 4, (j % 4) * 128:(j % 4 + 1) * 128],
                                      ktok[:, 2 * j:2 * j + 2, :].rearrange("p h d -> p (h d)"), ident)
                    if j % (HP // 2) == HP // 2 - 1:
                        mm.then_inc(S["ktp"], 1)
                if p >= 1:
                    heads_turned(p - 1)
                if p >= 1:
                    ctx_scores(2 * p + 1)
                    attn_out(p - 1)
                if p >= 2:
                    y3_transpose(p - 2)
                if p == 0:
                    keep_warm(WARM_KT)
                pe.wait_ge(S["qT"], p + 1)
                if p == 0:
                    pe.wait_ge(S["idm"], 2)
                for o in range(2):
                    r = slice(64 * o, 64 * o + SLOT)
                    for j in range(HP):
                        if o == 0 and j % (HP // 2) == 0:
                            pe.wait_ge(S["kT"], 2 * p + 1 + j // (HP // 2))
                        for i in range(2):
                            mm = pe.matmul(RA[i * SLOT:(i + 1) * SLOT, o, j * T:(j + 1) * T],
                                           qT[r, j, i * SLOT:(i + 1) * SLOT], kT[r, j, i * SLOT:i * SLOT + T],
                                           start=(j == 0), stop=False)
                    mm = pe.matmul(RA[:, o, 0:HP * T], identr[:, :], maskr[:, :].unsqueeze(1).broadcast_to([128, HP, T]),
                                   start=False, stop=True)
                    mm.then_inc(S["sc"], 1)
                    if o == 0:
                        ctx_sums(2 * p, 0)
                if p >= 1:
                    y2_transpose(p - 1)
                ctx_sums(2 * p, 1)
                if p >= 1:
                    query_features(p - 1)
                if p < PAIRS - 1:
                    ctx_scores(2 * p + 2)
                    queries(p + 1)
                if p >= 1:
                    cross_out(p - 1)
                pe.wait_ge(S["prb"], 2 * (p + 1))
                for j in range(HP):
                    mm = pe.transpose(RB[:, j // 4, (j % 4) * 128:(j % 4 + 1) * 128],
                                      pr[:, j, :, :].rearrange("p o t -> p (o t)"), ident)
                    if j % (HP // 2) == HP // 2 - 1:
                        mm.then_inc(S["ptp"], 1)
                ctx_sums(2 * p + 1, 0)
                if p < PAIRS - 1:
                    rope_keys(p + 1)
                    content_keys(p + 1)
                if p == 0:
                    pe.wait_ge(S["vv"], 1)
                if p >= 1:
                    pe.wait_ge(S["x1"], p)
                for j in range(HP):
                    if j % (HP // 2) == 0:
                        pe.wait_ge(S["pT"], 2 * p + 1 + j // (HP // 2))
                    for i in range(2):
                        mm = pe.matmul(M0[i * SLOT:(i + 1) * SLOT, j * 2 * VW:(j + 1) * 2 * VW],
                                       pT[:, j, i * SLOT:(i + 1) * SLOT], vv[:, 2 * p + i, j, :], start=True, stop=True)
                mm.then_inc(S["pv"], 1)
                if p < PAIRS - 1:
                    queries_turned(p + 1)
                    ctx_sums(2 * p + 1, 1)
            y3_transpose(PAIRS - 2)
            heads_turned(PAIRS - 1)
            ctx_sums(B - 1, 1)
            attn_out(PAIRS - 1)

            def product_high(bank, wh, wl, xh, first):
                pe.matmul(bank, wh, xh, start=first, stop=False)
                pe.matmul(bank, wl, xh, start=False, stop=False)

            def product_low(bank, wh, xl, last):
                return pe.matmul(bank, wh, xl, start=False, stop=last)

            def tokens(a, b0, b1):
                return a.rearrange("p q (i t) -> p (q i) t", i=2)[:, b0:b1, 0:T]

            def up_high(c, b0, b1):
                if c % PIECE == 0:
                    pe.wait_ge(S["wl"], c // PIECE + 1)
                product_high(ubank[c % UB][:, b0 * T:b1 * T], wuh[:, c, :], wul[:, c, :], tokens(y3h[:, :, :], b0, b1), True)

            def up_low(c, b0, b1):
                return product_low(ubank[c % UB][:, b0 * T:b1 * T], wuh[:, c, :], tokens(y3l[:, :, :], b0, b1), True)

            def up(c):
                if c >= UB:
                    pe.wait_ge(S["h"], nth(c - UB) + 1)
                up_high(c, 0, B)
                up_low(c, 0, B).then_inc(S["up"], 1)

            def router(p):
                return pe.matmul(M0[:, p * E:(p + 1) * E], y3T[:, p, :], col("router"), start=True, stop=True)

            def down(n):
                c, t = piece(n), span(n)
                e, j = divmod(c, CHUNKS)
                if j == 0 and e >= 2:
                    pe.wait_ge(S["acc0"], 1) if e == 2 else pe.wait_ge(S["ot"], e - 2)
                if c % PIECE == 0:
                    pe.wait_ge(S["wl"], NPC + c // PIECE + 1)
                pe.wait_ge(S["hh"], n + 1)
                bank = obank[e % 2][:, t]
                last = j == CHUNKS - 1
                product_high(bank, wdh[:, c, :], wdl[:, c, :], hh[:, c % 4, t], j == 0 and n != nth(0))
                wait_low(pe, n)
                mm = product_low(bank, wdh[:, c, :], hl[:, c % 4, t], last)
                if n >= AHEAD:
                    mm.then_inc(S["dn"], 1)

            p, done = PAIRS - 1, B - 2
            for c in range(4):
                up_high(c, 0, done)
            pe.wait_ge(S["y3l"], p)
            for c in range(4):
                mm = up_low(c, 0, done)
                if c < AHEAD:
                    mm.then_inc(S["up"], 1)
            y2_transpose(p)
            for q in range(p):
                router(q)
            query_features(p)
            pe.wait_ge(S["kvs"], B)
            keep_warm(WARM_RFQ)
            cross_out(p)
            for n in range(AHEAD - 1):
                down(n)
            keep_warm(WARM_Y3)
            y3_transpose(p)
            down(AHEAD - 1)
            pe.wait_ge(S["y3T"], 2 * PAIRS)
            router(p).then_inc(S["lg"], 1)
            for c in range(4):
                up_high(c, done, B)
                if c == 0:
                    pe.wait_ge(S["y3l"], PAIRS)
                up_low(c, done, B).then_inc(S["up"], 1)
            pe.wait_ge(S["en"], 1)
            up(UB - 1)
            def back(p, src, first=False, last=False):
                return pe.matmul(fbank[p // 2][:, p % 2, :], src[:, 2 * p:2 * p + 2, :].rearrange("p b t -> p (b t)"), ident,
                                 start=first, stop=last)

            for c in range(NCH):
                down(nth(c))
                if c + UB < NCH:
                    up(c + UB)
                if c == 3:
                    pe.wait_ge(S["cmb"], 1)
                    for p in range(PAIRS):
                        mm = pe.transpose(X0[0:E, p * 128:(p + 1) * 128], sel[:, 4, p, :], ident)
                    mm.then_inc(S["cmtp"], 1)
            pe.wait_ge(S["accp"], E - 1)
            for p in range(PAIRS):
                back(p, acc, first=(p % 2 == 0))
            for k in range(2):
                pe.wait_ge(S["ot"], E + k)
                for p in (2 * k, 2 * k + 1):
                    mm = back(p, end, last=(p % 2 == 1))
                mm.then_inc(S["ftp"], 1)

        @block.scalar
        def _(act):
            def copy(dst, src, after, n, done, scale=1.0):
                act.wait_ge(S[after], n)
                act.activation(dst, src, ACT.Copy, scale=scale).then_inc(S[done], 1)

            def flat(a):
                return a.rearrange("p a b -> p (a b)")

            def ctx_exp(b):
                act.wait_ge(S["cs"], b + 1)
                if b >= 1:
                    act.wait_ge(S["rft"], b)
                act.activation(rf[:, :], C0[:, 0:GL], ACT.Exp,
                               scale=float(D) ** -0.5).then_inc(S["rf"], 1)

            def ctx_low(b):
                if b >= 1:
                    act.wait_ge(S["kvs"], b)
                copy(kvl[:, :], K0[M:2 * M, 0:2 * CW], "ck", b + 1, "kvl")

            def ctx_high(b):
                act.wait_ge(s_cn[b % RING], 16 * (b // RING + 1))
                if b >= 2:
                    act.wait_ge(S["ck"], b - 1)
                act.activation(ctxsv[:, b % 2, :, 0, :], tiles(b), ACT.Copy).then_inc(S["ch"], 1)

            def weights_high(k):
                act.wait_ge(s_w[k % 2], 16 * (k // 2 + 1))
                j = k % NPC
                act.activation((wuh if k < NPC else wdh)[:, j * PIECE:(j + 1) * PIECE, :], wraw[:, k % 2, :, :],
                               ACT.Copy).then_inc(S["wh"], 1)

            def y3_copies(p):
                copy(y3T[:, p, :], X0[:, 0:128], "y3tp", p + 1, "y3T")
                copy(y3h[:, p, :], X0[:, 0:128], "y3tp", p + 1, "y3T")

            def query_exp(p):
                act.wait_ge(S["rfqp"], p + 1)
                if p >= 1:
                    act.wait_ge(S["xo"], p)
                act.activation(rfq[:, :], X0[0:M, 128:256], ACT.Exp, scale=float(D) ** -0.5).then_inc(S["rfq"], 1)

            copy(flat(yT[:, :, :]), M0[:, :], "yT", 1, "qc")
            ctx_exp(0)
            copy(flat(qcT[:, :, :]), RA[0:QR, 0, :], "kvtok", 2, "kvnT")
            act.wait_ge(s_inB, 48)
            copy(flat(kvnT[:, :, :]), M0[0:KVR, :], "kvtp", 1, "kvnT", scale=p32[:, 256:257])
            def turned_queries(p):
                if p >= 1:
                    act.wait_ge(S["sc"], 2 * p)
                copy(flat(qT[:, :, :]), flat(RA[:, :, :]), "qtp", p + 1, "qT")

            ctx_high(0)
            def half(dst, g, after, p, done):
                copy(flat(dst[:, g * HP // 2:(g + 1) * HP // 2, :]), RB[:, g, :], after, 2 * p + g + 1, done)

            def probabilities(p, o):
                if o == 0:
                    act.wait_ge(S["pads"], 2)
                    if p >= 1:
                        act.wait_ge(S["ptp"], 2 * p)
                act.wait_ge(S["sub"], 2 * p + o + 1)
                act.activation(pr[:, :, o, 0:T], sm[:, o, :, :], ACT.Exp, scale=float(QK) ** -0.5).then_inc(S["prb"], 1)

            turned_queries(0)
            for p in range(PAIRS):
                if p >= 1:
                    act.wait_ge(S["sc"], 2 * p)
                if p >= 1:
                    copy(atT[:, :], M0[:, 144:272], "atp", p, "atT")
                half(kT, 0, "ktp", p, "kT")
                half(kT, 1, "ktp", p, "kT")
                ctx_exp(2 * p + 1)
                ctx_high(2 * p + 1)
                if p < PAIRS - 1:
                    weights_high(PPP * p)
                if p >= 2:
                    y3_copies(p - 2)
                probabilities(p, 0)
                if p >= 1:
                    copy(y2T[:, :], X0[:, 0:128], "y2tp", p, "y2T")
                    query_exp(p - 1)
                ctx_low(2 * p)
                probabilities(p, 1)
                if p < PAIRS - 1:
                    weights_high(PPP * p + 1)
                if p >= 1:
                    act.wait_ge(S["pv"], p)
                half(pT, 0, "ptp", p, "pT")
                half(pT, 1, "ptp", p, "pT")
                if p < PAIRS - 1:
                    ctx_exp(2 * p + 2)
                    ctx_high(2 * p + 2)
                    turned_queries(p + 1)
                    ctx_low(2 * p + 1)
                    weights_high(PPP * p + 2)
            def relu(n):
                c, t = piece(n), span(n)
                act.wait_ge(S["up"], n + 1)
                if n >= 2:
                    act.wait_ge(S["h"], n - 1)
                act.activation(rl[n % 2][:, t], ubank[c % UB][:, t], ACT.Relu).then_inc(S["rl"], 1)

            def hidden_high(n):
                c, t = piece(n), span(n)
                act.wait_ge(S["h"], n + 1)
                if c >= 4:
                    act.wait_ge(S["dn"], c - 3)
                act.activation(hh[:, c % 4, t], hf[:, c % 4, t], ACT.Copy).then_inc(S["hh"], 1)

            p = PAIRS - 1
            y3_copies(p - 1)
            copy(atT[:, :], M0[:, 144:272], "atp", p + 1, "atT")
            ctx_low(2 * p + 1)
            relu(0)
            relu(1)
            copy(y2T[:, :], X0[:, 0:128], "y2tp", p + 1, "y2T")
            hidden_high(0)
            query_exp(p)
            for n in range(2, AHEAD):
                relu(n)
                hidden_high(n - 1)
            hidden_high(AHEAD - 1)
            y3_copies(p)
            relu(nth(0))
            act.wait_ge(S["lg"], 1)
            act.activation(gate[:, 0, :, :], M0[:, 0:PAIRS * E].rearrange("p (q e) -> p q e", q=PAIRS), ACT.Exp,
                           scale=-1.0).then_inc(S["en"], 1)
            for c in range(1, NCH):
                relu(nth(c))
                hidden_high(nth(c - 1))
                if c in LATE_AT:
                    weights_high(2 * NPC - LATE + LATE_AT.index(c))
                if c == 6:
                    copy(flat(cT[:, :, :]), X0[0:E, :], "cmtp", 1, "cT")
            hidden_high(nth(NCH - 1))

        @block.gpsimd
        def _(pool):
            pool.memset(mhalf[:, :], -0.5)
            pool.memset(vv[:, :, :, :], 0.0).then_inc(S["pads"], 1)
            pool.memset(qtok[:, :, QK:SLOT], 0.0)
            pool.memset(ktok[:, :, QK:SLOT], 0.0)
            pool.memset(pr[:, :, :, T:SLOT], 0.0).then_inc(S["pads"], 1)

            def power(dst, src, after, n, done):
                pool.wait_ge(S[after], n)
                pool.tensor_tensor(dst, src, mhalf[:, 0:src.shape[1]], ALU.pow).then_inc(S[done], 1)

            pool.wait_ge(S["pads"], 2)
            power(rstd[:, 0, :], vpe[:, 0, :], "ln_eps", 1, "ln_pow")
            power(kvrs[:, :], kvms[:, :], "kvms", 1, "kvpow")

            def low(dst, src, high, done):
                pool.tensor_tensor(dst, src, high.bitcast(F32), ALU.subtract).then_inc(S[done], 1)

            def ctx_lows(b):
                pool.wait_ge(S["ch"], b + 1)
                low(ctxsv[:, b % 2, :, 1, :], tiles(b), ctxsv[:, b % 2, :, 0, :], "cl")

            def weights_low(k):
                pool.wait_ge(S["wh"], k + 1)
                h, l = (wuh, wul) if k < NPC else (wdh, wdl)
                j = k % NPC
                low(l[:, j * PIECE:(j + 1) * PIECE, :], wraw[:, k % 2, :, :], h[:, j * PIECE:(j + 1) * PIECE, :], "wl")

            def ln_power(k, p):
                power(rstd[:, k, p:p + 1], vpe[:, k, p:p + 1], "ln_eps", 2 * p + k + 1, "ln_pow")

            ctx_lows(0)
            for p in range(PAIRS):
                if p >= 1:
                    ln_power(1, p - 1)
                ctx_lows(2 * p + 1)
                if p < PAIRS - 1:
                    weights_low(PPP * p)
                    weights_low(PPP * p + 1)
                if p >= 1:
                    ln_power(2, p - 1)
                if p < PAIRS - 1:
                    ctx_lows(2 * p + 2)
                    weights_low(PPP * p + 2)

            def hidden_low(n):
                c, t = piece(n), span(n)
                if not on_pool(c):
                    return
                pool.wait_ge(S["hh"], n + 1)
                if c >= 4:
                    pool.wait_ge(S["dn"], c - 3)
                low(hl[:, c % 4, t], hf[:, c % 4, t], hh[:, c % 4, t], "hlp")

            ln_power(1, PAIRS - 1)
            for n in range(AHEAD):
                hidden_low(n)
            ln_power(2, PAIRS - 1)

            def add_expert(e):
                pool.wait_ge(S["ot"], e)
                if e == 1:
                    pool.wait_ge(S["acc0"], 1)
                else:
                    pool.wait_ge(S["accp"], e - 1)
                pool.tensor_tensor(accv, accv, ot[:, e % 2, :].rearrange("p (b t) -> p b t", b=B),
                                   ALU.add).then_inc(S["accp"], 1)

            for c in range(NCH):
                hidden_low(nth(c))
                if c % CHUNKS == CHUNKS - 1 and c >= 3 * CHUNKS - 1:
                    add_expert(c // CHUNKS - 1)
                if c in LATE_AT:
                    weights_low(2 * NPC - LATE + LATE_AT.index(c))

        @block.vector
        def _(v):
            count = {}

            def step(ins, name):
                ins.then_inc(S[name], 1)
                count[name] = count.get(name, 0) + 1

            def own(name):
                v.wait_ge(S[name], count[name])

            def bcast(a, shape):
                return a.unsqueeze(len(a.shape)).broadcast_to(shape)

            def high(dst, src):
                return v.tensor_copy(dst, src)

            def low(dst, src, h):
                return v.tensor_tensor(dst, src, h.bitcast(F32), ALU.subtract)

            def features_turned(b):
                v.wait_ge(S["rf"], b + 1)
                if b >= 1:
                    own("rfs")
                step(v.transpose(rft[:, :, :].rearrange("p j m -> p (j m)"), rf[:, :]), "rft")

            def features_high(b):
                if b >= 1:
                    v.wait_ge(S["ck"], b)
                own("rft")
                step(high(rfs[:, :, 0, :], rft[:, :, :]), "fh")

            def features_low(b):
                own("fh")
                step(low(rfs[:, :, 1, :], rft[:, :, :], rfs[:, :, 0, :]), "rfs")

            def ctx_total_features(b):
                v.wait_ge(S["kvl"], b + 1)
                step(v.tensor_tensor(kvh[:, :], K0[0:M, 0:2 * CW], kvl[:, :], ALU.add), "kvh")

            def ctx_total(b):
                own("kvh")
                step(v.tensor_tensor(kvs[:, b, :], kvh[:, 0:D + 1], kvh[:, CW:CW + D + 1], ALU.add), "kvs")

            def y3_low(p):
                v.wait_ge(S["y3T"], 2 * p + 2)
                step(low(y3l[:, p, :], y3T[:, p, :], y3h[:, p, :]), "y3l")

            def ln_stats(x, k, p):
                step(v.bn_stats(stats[:, k, p, :], x), "ln_stat")

            def ln_mean(k, p):
                own("ln_stat")
                step(v.bn_aggr(mv[:, k, p, :], stats[:, k, p, :]), "ln_mean")

            def ln_eps(k, p0, p1):
                own("ln_mean")
                step(v.tensor_scalar(vpe[:, k, p0:p1], mv[:, k, p0:p1, 1], LN_EPS, None, ALU.add), "ln_eps")

            def ln_apply(dst, x, k, p):
                return v.tensor_scalar(dst, x, mv[:, k, p, 0:1], rstd[:, k, p:p + 1], ALU.subtract, ALU.mult)

            v.wait_ge(s_x, 16)
            for p in range(PAIRS):
                ln_stats(xin[:, p, :], 0, p)
            for p in range(PAIRS):
                ln_mean(0, p)
            ln_eps(0, 0, PAIRS)
            v.wait_ge(S["ln_pow"], 1)
            for p in range(PAIRS):
                step(ln_apply(y1[:, p, :], xin[:, p, :], 0, p), "y1")
            v.wait_ge(s_inA, 16)
            step(high(identr[:, :], ident), "idm")
            v.wait_ge(S["kvtok"], 1)
            step(v.tensor_copy(kvt[:, :, :].rearrange("p a b -> p (a b)"), X0[:, 0:PAIRS * KVR]), "kvcp")
            own("kvcp")
            step(v.tensor_tensor(kvsq[:, :, :], kvt[:, :, :], kvt[:, :, :], ALU.mult), "kvsq")
            own("kvsq")
            step(v.tensor_reduce(kvss[:, :], kvsq[:, :, :], AX_X, ALU.add), "kvss")
            own("kvss")
            step(v.tensor_scalar(kvms[:, :], kvss[:, :], 1.0 / KVR, RMS_EPS, ALU.mult, ALU.add), "kvms")
            v.wait_ge(S["kvpow"], 1)
            step(v.tensor_tensor(kvn[:, :, :], kvt[:, :, :], bcast(kvrs[:, :], [128, PAIRS, KVR]), ALU.mult), "kvn")
            v.wait_ge(S["pads"], 2)
            v.memset(vv[0:64, :, :, HD:HD + 1], 1.0)
            v.memset(vv[64:128, :, :, VW + HD:VW + HD + 1], 1.0)

            def heads(region):
                return region[:, :, 0:8 * QK].rearrange("p g (h d) -> p g h d", h=8)

            c4 = [128, 2, 8, RD]
            half = [128, 2, 8, RD // 2]
            cosed, sined = (a[:, :, :].rearrange("p (g h) d -> p g h d", g=2) for a in rt)

            def table(name, a, b, shape):
                return col(name)[:, a:b].unsqueeze(1).unsqueeze(1).broadcast_to(shape)

            def times_cos(region):
                v.tensor_tensor(cosed, heads(region)[:, :, :, HD:QK], table("cos", 0, RD, c4), ALU.mult)

            def times_sin(region, k, done):
                a, b = (0, 16) if k == 0 else (16, 0)
                step(v.tensor_tensor(sined[:, :, :, a:a + 16], heads(region)[:, :, :, HD + b:HD + b + 16],
                                     table("sin", a, a + 16, half), ALU.mult), done)

            def content(region, tok, done):
                th = tok[:, :, :].rearrange("p (g h) d -> p g h d", g=2)
                step(v.tensor_copy(th[:, :, :, 0:HD], heads(region)[:, :, :, 0:HD]), done)

            def query_sum():
                own("rq")
                step(v.tensor_tensor(qtok[:, :, HD:QK], rt[0][:, :, :], rt[1][:, :, :], ALU.add), "qadd")

            def attn_sums(p):
                v.wait_ge(S["pv"], p + 1)
                step(v.reciprocal(rs[:, :], M0[:, 0:HP * 2 * VW].rearrange("p (h d) -> p h d", h=H)[:, :, HD]), "rsum")

            def attn_norm(p):
                own("rsum")
                if p >= 1:
                    v.wait_ge(S["atp"], p)
                step(v.tensor_tensor(at[:, :, :], M0[:, 0:HP * 2 * VW].rearrange("p (h d) -> p h d", h=H)[:, :, 0:HD],
                                     bcast(rs[:, :], [128, H, HD]), ALU.mult), "atn")

            def residual1(p):
                v.wait_ge(S["wo"], p + 1)
                step(v.tensor_tensor(x1[:, p, :], M0[:, 272:400], xin[:, p, :], ALU.add), "x1")

            def stats1(p):
                own("x1")
                ln_stats(x1[:, p, :], 1, p)

            def norm2(p):
                v.wait_ge(S["ln_pow"], 2 * p + 2)
                if p >= 1:
                    v.wait_ge(S["y2tp"], p)
                step(ln_apply(y2[:, :], x1[:, p, :], 1, p), "y2")

            def cross_sums(p):
                v.wait_ge(S["xo"], p + 1)
                step(v.tensor_scalar(den[:, 0:1], X0[:, 256 + D:257 + D], XN_EPS * float(M) ** 0.5, None, ALU.add), "den")

            def cross_recip():
                own("den")
                step(v.reciprocal(den[:, 1:2], den[:, 0:1]), "drec")

            def residual2(p):
                own("drec")
                step(v.scalar_tensor_tensor(out=x2[:, p, :], in0=X0[:, 256:256 + D], scalar=den[:, 1:2], in1=x1[:, p, :],
                                            op0=ALU.mult, op1=ALU.add), "x2")

            def stats2(p):
                own("x2")
                ln_stats(x2[:, p, :], 2, p)

            def norm3(p):
                v.wait_ge(S["ln_pow"], 2 * p + 3)
                if p >= 1:
                    v.wait_ge(S["y3tp"], p)
                step(ln_apply(y3[:, :], x2[:, p, :], 2, p), "y3")

            v.wait_ge(s_inB, 48)
            step(high(maskr[:, :], col("mask")), "idm")
            v.wait_ge(S["pq"], 1)
            times_cos(RA)
            times_sin(RA, 0, "rq")
            times_sin(RA, 1, "rq")
            content(RA, qtok, "rq")
            query_sum()
            for p in range(PAIRS):
                own("qadd")
                if p >= 1:
                    v.wait_ge(S["ktp"], 2 * p)
                v.wait_ge(S["pk"], p + 1)
                times_cos(RB)
                if p >= 2:
                    norm3(p - 2)
                times_sin(RB, 0, "rk")
                if p >= 1:
                    attn_sums(p - 1)
                times_sin(RB, 1, "rk")
                if p >= 1:
                    attn_norm(p - 1)
                content(RB, ktok, "rk")
                own("rk")
                for g in range(2):
                    heads_g = slice(g * H // 2, (g + 1) * H // 2)
                    step(v.tensor_tensor(ktok[:, heads_g, HD:QK], rt[0][:, heads_g, :], rt[1][:, heads_g, :], ALU.add), "kadd")
                if p >= 1:
                    ctx_total_features(2 * p - 1)
                features_turned(2 * p)
                if p >= 1:
                    ctx_total(2 * p - 1)
                features_high(2 * p)
                features_low(2 * p)
                if p == 0:
                    v.wait_ge(S["v"], 1)
                    for o in range(2):
                        src = M0[64 * o:64 * o + 64, :].rearrange("p (b j d) -> p b j d", b=B, j=HP)
                        ins = v.tensor_copy(vv[64 * o:64 * o + 64, :, :, o * VW:o * VW + HD], src)
                    step(ins, "vv")
                if p >= 1:
                    residual1(p - 1)
                    stats1(p - 1)
                    ln_mean(1, p - 1)
                    ln_eps(1, p - 1, p)
                if p >= 1:
                    v.wait_ge(S["prb"], 2 * p)
                wide = [128, HP, T]
                for o in range(2):
                    v.wait_ge(S["sc"], 2 * p + o + 1)
                    scores = RA[:, o, 0:HP * T].rearrange("p (j t) -> p j t", j=HP)
                    step(v.tensor_reduce(mx[:, o, :], scores, AX_X, ALU.max), "smx")
                    own("smx")
                    step(v.tensor_tensor(sm[:, o, :, :], scores, bcast(mx[:, o, :], wide), ALU.subtract), "sub")
                    if o == 0 and p >= 1:
                        norm2(p - 1)
                features_turned(2 * p + 1)
                ctx_total_features(2 * p)
                features_high(2 * p + 1)
                ctx_total(2 * p)
                features_low(2 * p + 1)
                if p < PAIRS - 1:
                    v.wait_ge(S["pq"], p + 2)
                    v.wait_ge(S["qtp"], p + 1)
                    own("kadd")
                    times_cos(RA)
                if p >= 1:
                    cross_sums(p - 1)
                if p < PAIRS - 1:
                    times_sin(RA, 0, "rq")
                if p >= 1:
                    cross_recip()
                if p < PAIRS - 1:
                    times_sin(RA, 1, "rq")
                if p >= 1:
                    residual2(p - 1)
                if p < PAIRS - 1:
                    content(RA, qtok, "rq")
                if p >= 1:
                    stats2(p - 1)
                if p < PAIRS - 1:
                    query_sum()
                if p >= 2:
                    y3_low(p - 2)
                if p >= 1:
                    ln_mean(2, p - 1)
                    ln_eps(2, p - 1, p)
            def hidden(n):
                c, t = piece(n), span(n)
                v.wait_ge(S["rl"], n + 1)
                if c >= 4:
                    v.wait_ge(S["hh"], nth(c - 4) + 1)
                    wait_low(v, nth(c - 4))
                step(v.scalar_tensor_tensor(out=hf[:, c % 4, t], in0=ubank[c % UB][:, t], scalar=0.0, in1=rl[n % 2][:, t],
                                            op0=ALU.max, op1=ALU.mult), "h")

            def hidden_low(n):
                c, t = piece(n), span(n)
                if on_pool(c):
                    return
                v.wait_ge(S["hh"], n + 1)
                if c >= 4:
                    v.wait_ge(S["dn"], c - 3)
                step(low(hl[:, c % 4, t], hf[:, c % 4, t], hh[:, c % 4, t]), "hlv")

            p = PAIRS - 1
            norm3(p - 1)
            attn_sums(p)
            attn_norm(p)
            residual1(p)
            stats1(p)
            ln_mean(1, p)
            ln_eps(1, p, p + 1)
            y3_low(p - 1)
            norm2(p)
            ctx_total_features(2 * p + 1)
            ctx_total(2 * p + 1)
            hidden(0)
            hidden(1)
            hidden_low(0)
            cross_sums(p)
            cross_recip()
            residual2(p)
            stats2(p)
            ln_mean(2, p)
            ln_eps(2, p, p + 1)
            for n in range(2, AHEAD):
                hidden(n)
            norm3(p)
            for n in range(2, AHEAD):
                hidden_low(n)
            y3_low(p)

            def tok(a):
                return a.rearrange("p (b t) -> p b t", b=B)

            def expert_out(e):
                v.wait_ge(S["dn"], CHUNKS * (e + 1))
                if e == 0:
                    step(v.tensor_copy(accv, tok(obank[0][:, 0:NT])), "acc0")
                    return
                v.wait_ge(s_cb[e > 2], 16 * (2 if e <= 2 else E - 2))
                if e == E:
                    for k in range(2):
                        b = slice(k * B // 2, (k + 1) * B // 2)
                        step(v.tensor_tensor(end[:, b, 0:T], tok(obank[e % 2][:, 0:NT])[:, b, :], tok(cb[:, e - 1, :])[:, b, :],
                                             ALU.mult), "ot")
                    return
                if e >= 3:
                    v.wait_ge(S["accp"], e - 2)
                step(v.tensor_tensor(ot[:, e % 2, :], obank[e % 2][:, 0:NT], cb[:, e - 1, :], ALU.mult), "ot")

            shape = [128, PAIRS, E]

            def choose_probs():
                v.memset(acc[:, :, T:SLOT], 0.0)
                v.wait_ge(S["en"], 1)
                step(v.tensor_scalar(gate[:, 1, :, :], gate[:, 0, :, :], 1.0, None, ALU.add), "one")
                own("one")
                step(v.reciprocal(gate[:, 2, :, :], gate[:, 1, :, :]), "prbs")

            def choose_top():
                own("prbs")
                for p in range(PAIRS):
                    step(v.max(top[:, p, :], gate[:, 2, p, :]), "topv")
                own("topv")
                for p in range(PAIRS):
                    step(v.max_index(topi[:, p, :], top[:, p, :], gate[:, 2, p, :]), "topx")

            def choose_share():
                own("topx")
                step(v.tensor_copy(topf[:, :, :], topi[:, :, 0:2]), "topf")
                step(v.tensor_tensor(tden[:, 0, :], top[:, :, 0], top[:, :, 1], ALU.add), "dsum")
                own("dsum")
                step(v.tensor_scalar(tden[:, 1, :], tden[:, 0, :], TOPK_EPS, None, ALU.add), "dsum")
                own("dsum")
                step(v.reciprocal(tden[:, 2, :], tden[:, 1, :]), "drc")
                own("topf")
                iota = col("iota").unsqueeze(1).broadcast_to(shape)
                for k in range(2):
                    step(v.tensor_tensor(sel[:, k, :, :], iota, bcast(topf[:, :, k], shape), ALU.is_equal), "selc")

            def choose_weights():
                own("selc")
                for k in range(2):
                    step(v.tensor_tensor(sel[:, 2 + k, :, :], sel[:, k, :, :], bcast(top[:, :, k], shape), ALU.mult), "selc")
                own("selc")
                step(v.tensor_tensor(sel[:, 0, :, :], sel[:, 2, :, :], sel[:, 3, :, :], ALU.add), "selc")
                own("selc")
                own("drc")
                step(v.tensor_tensor(sel[:, 4, :, :], sel[:, 0, :, :], bcast(tden[:, 2, :], shape), ALU.mult), "cmb")

            for c in range(NCH):
                hidden(nth(c))
                if c == NCH - 1:
                    expert_out(c // CHUNKS - 1)
                if c >= 1:
                    hidden_low(nth(c - 1))
                if 1 <= c <= 4:
                    (choose_probs, choose_top, choose_share, choose_weights)[c - 1]()
                if c % CHUNKS == CHUNKS - 1 and CHUNKS < c < NCH - 1:
                    expert_out(c // CHUNKS - 1)
            hidden_low(nth(NCH - 1))
            expert_out(E)
            for k in range(2):
                v.wait_ge(S["ftp"], k + 1)
                step(v.tensor_tensor(fin[:, 2 * k:2 * k + 2, :], fbank[k],
                                     x2[:, 2 * k:2 * k + 2, :], ALU.add), "fin")


def _constants():
    mask = np.zeros((2, SLOT, T), np.float32)
    mask[:, :T] = np.where(np.tril(np.ones((T, T), bool)), 0.0, NEG)
    inv_freq = 1.0 / 10000.0 ** (np.arange(0, RD, 2, dtype=np.float32) / RD)
    freqs = np.outer(np.arange(T, dtype=np.float32), inv_freq)
    cos, sin = np.zeros((2, SLOT, RD), np.float32), np.zeros((2, SLOT, RD), np.float32)
    cos[:, :T] = np.cos(np.concatenate([freqs, freqs], -1))
    sin[:, :T] = np.sin(np.concatenate([-freqs, freqs], -1))
    return {
        "ident": np.eye(128, dtype=np.float32), "mask": mask.reshape(128, T), "cos": cos.reshape(128, RD),
        "sin": sin.reshape(128, RD), "iota": np.tile(np.arange(E, dtype=np.float32), (128, 1)),
    }


def kernel(x, ctx_1024, L0_attn_W_kv, L0_attn_g_kv, L0_attn_W_kdec, L0_attn_W_vdec, L0_attn_W_q, L0_attn_W_qdec,
           L0_attn_W_krope, L0_attn_W_qrope, L0_attn_W_o, L0_xattn_projection, L0_ffn_W_router, L0_ffn_W_up,
           L0_ffn_W_down, L0_ffn_W_sh_up, L0_ffn_W_sh_down):
    import concourse.bacc as _bacc
    from concourse.bass_utils import run_bass_kernel_spmd as _run

    a = {k: np.asarray(v) for k, v in locals().items() if k[0] != "_"}
    xp = np.zeros((PAIRS, 2, SLOT, D), np.float32)
    xp[:, :, :T] = a["x"].reshape(PAIRS, 2, T, D)
    parts = _constants() | {
        "xpad": xp.reshape(PAIRS, 128, D).transpose(1, 0, 2).reshape(128, PAIRS * D),
        "wkv": a["L0_attn_W_kv"], "wq": a["L0_attn_W_q"], "krope": a["L0_attn_W_krope"], "wo": a["L0_attn_W_o"],
        "proj": a["L0_xattn_projection"].T, "router": a["L0_ffn_W_router"],
    }
    pack128 = np.concatenate([parts[k] for k in W128], 1)
    wqcat = np.concatenate([a["L0_attn_W_qdec"].reshape(QR, H, HD), a["L0_attn_W_qrope"].reshape(QR, H, RD)], 2)
    pack32 = np.concatenate([a["L0_attn_W_kdec"], a["L0_attn_W_vdec"], a["L0_attn_g_kv"].reshape(KVR, 1)], 1)
    c = np.zeros((B, GR * GL, CW), np.float32)
    c[:, :L, :D] = a["ctx_1024"]
    c[:, :L, D:] = 1.0
    ctx_nat = c.reshape(B, GR, CT, 32, CW).transpose(0, 1, 3, 2, 4).reshape(B, 128, CT * CW)
    ctx_tr = c[:, :, :D].transpose(0, 2, 1).reshape(B, D, GR, GL)
    up = np.concatenate([a["L0_ffn_W_sh_up"][None], a["L0_ffn_W_up"]], 0).reshape(E + 1, D, CHUNKS, 128)
    down = np.concatenate([a["L0_ffn_W_sh_down"][None], a["L0_ffn_W_down"]], 0).reshape(NCH, 128, D)
    arrays = {
        "pack128": pack128, "wqcat": wqcat.reshape(QR, H * QK), "pack32": pack32, "ctx_nat": ctx_nat, "ctx_tr": ctx_tr,
        "w_up": up.transpose(1, 0, 2, 3).reshape(D, NCH, 128), "w_down": down.transpose(1, 0, 2),
    }
    arrays = {k: np.ascontiguousarray(v) for k, v in arrays.items()}
    nc = _bacc.Bacc("TRN2", target_bir_lowering=False, num_devices=1)
    args = [nc.dram_tensor(k, v.shape, mybir.dt.from_np(v.dtype), kind="ExternalInput").ap() for k, v in arrays.items()]
    out = nc.dram_tensor("out", (128, PAIRS, D), F32, kind="ExternalOutput").ap()
    share = nc.dram_tensor("share", (E, B, T), F32, kind="Internal").ap()
    decoder_layer(nc, *args, share, out)
    got = _run(nc, [arrays], core_ids=[0]).results[0]["out"]
    return got.reshape(2, SLOT, PAIRS, D).transpose(2, 0, 1, 3)[:, :, :T].reshape(B, T, D)
```
